# Optimizing a Trainium2 kernel written in Bass

```python
import numpy as np
import jax
import jax.numpy as jnp

def _softmax(x, axis=-1):
    return jax.nn.softmax(x, axis=axis)

def _gelu(x):
    return jax.nn.gelu(x, approximate=True)

def _silu(x):
    return jax.nn.silu(x)

def _sigmoid(x):
    return jax.nn.sigmoid(x)

def _layernorm(x, axis=-1, eps=1e-05):
    m = jnp.mean(x, axis=axis, keepdims=True)
    v = jnp.var(x, axis=axis, keepdims=True)
    return (x - m) / jnp.sqrt(v + eps)

def _scatter_add(tgt, idx, src, axis=0):
    return tgt.at[idx].add(src)

def _segment_sum(src, seg, n):
    return jax.ops.segment_sum(src, seg, n)
kernel_name = 'mk_conv_attn_hybrid_d4_conv_nhwc256_r4_a59cac'

def setup_inputs(seed: int=0):
    np.random.seed(seed)
    _w = jnp.asarray

    def _rec_inputs():
        import jax
        import jax.numpy as jnp
        _gk = jax.random.key(seed)
        x = -0.0005207 + 1.001 * jax.random.normal(jax.random.fold_in(_gk, 1), (2, 16, 16, 64), jnp.float32)
        return x
    x = _rec_inputs()

    def _L0_conv_setup():
        import jax, jax.numpy as jnp
        import numpy as np
        DIM, K, NH = (64, 7, 8)

        def _nbhd_idx(n, k):
            start = jnp.clip(jnp.arange(n) - k // 2, 0, n - k)
            idx = start[:, None] + jnp.arange(k)[None, :]
            bias = idx - jnp.arange(n)[:, None] + (k - 1)
            return (idx, bias)
        key = jax.random.key(seed)
        ks = jax.random.split(key, 8)
        s = lambda k_, sh, fan: jax.random.normal(k_, sh, jnp.float32) * fan ** (-0.5)
        return {'x': jax.random.normal(ks[0], (2, 16, 16, DIM), jnp.float32), 'qkv_w': s(ks[1], (DIM, 3 * DIM), DIM), 'qkv_b': jnp.zeros((3 * DIM,), jnp.float32), 'rpb': 0.02 * jax.random.normal(ks[2], (NH, 2 * K - 1, 2 * K - 1), jnp.float32), 'proj_w': s(ks[3], (DIM, DIM), DIM), 'proj_b': jnp.zeros((DIM,), jnp.float32), 'g1_w': s(ks[4], (DIM, DIM // 4), DIM), 'g1_b': jnp.zeros((DIM // 4,), jnp.float32), 'g2_w': s(ks[5], (DIM // 4, 1), DIM // 4), 'g2_b': jnp.zeros((1,), jnp.float32), 'ln_g': jnp.ones((DIM,), jnp.float32), 'ln_b': jnp.zeros((DIM,), jnp.float32)}
    _L0_conv_all = _L0_conv_setup()
    _L0_conv_in = {k: v for k, v in _L0_conv_all.items() if k in ('qkv_w', 'qkv_b', 'rpb', 'proj_w', 'proj_b', 'g1_w', 'g1_b', 'g2_w', 'g2_b', 'ln_g', 'ln_b')}
    del _L0_conv_all

    def _L1_conv_setup():
        import jax, jax.numpy as jnp
        import numpy as np
        UNITS = 64
        GROUPS = 8
        EPS = 0.001

        def group_norm(x, gamma, beta, groups=GROUPS, eps=EPS):
            B, H, W, C = x.shape
            xg = x.reshape(B, H, W, groups, C // groups)
            mean = xg.mean(axis=(1, 2, 4), keepdims=True)
            var = xg.var(axis=(1, 2, 4), keepdims=True)
            xn = (xg - mean) * jax.lax.rsqrt(var + eps)
            xn = xn.reshape(B, H, W, C)
            return xn * gamma + beta
        key = jax.random.key(seed)
        ks = jax.random.split(key, 10)
        B, H, W, C = (4, 16, 16, UNITS)
        s = 1.0 / np.sqrt(C)
        x = jax.random.normal(ks[0], (B, H, W, C), dtype=jnp.float32)
        return {'x': x, 'gamma': jnp.ones((C,), jnp.float32), 'beta': jnp.zeros((C,), jnp.float32), 'Wq': jax.random.uniform(ks[1], (C, C), jnp.float32, -s, s), 'bq': jnp.zeros((C,), jnp.float32), 'Wk': jax.random.uniform(ks[2], (C, C), jnp.float32, -s, s), 'bk': jnp.zeros((C,), jnp.float32), 'Wv': jax.random.uniform(ks[3], (C, C), jnp.float32, -s, s), 'bv': jnp.zeros((C,), jnp.float32), 'Wp': jax.random.uniform(ks[4], (C, C), jnp.float32, -1e-05, 1e-05), 'bp': jnp.zeros((C,), jnp.float32)}
    _L1_conv_all = _L1_conv_setup()
    _L1_conv_in = {k: v for k, v in _L1_conv_all.items() if k in ('gamma', 'beta', 'Wq', 'bq', 'Wk', 'bk', 'Wv', 'bv', 'Wp', 'bp')}
    del _L1_conv_all

    def _L2_attn_setup():
        import jax, jax.numpy as jnp
        import numpy as np
        KERNEL_SIZE = 3
        DILATIONS = (1, 2, 3)

        def _window(t, dilation, ksize):
            B, N, C = t.shape
            pad = dilation * (ksize - 1) // 2
            tp = jnp.pad(t, ((0, 0), (pad, pad), (0, 0)))
            idx = jnp.arange(N)[:, None] + jnp.arange(ksize)[None, :] * dilation
            return tp[:, idx, :]
        key = jax.random.key(seed)
        k0, k1, k2 = jax.random.split(key, 3)
        B, N, C = (16, 1024, 64)
        x = jax.random.normal(k0, (B, N, C), jnp.float32)
        Wqkv = jax.random.normal(k1, (len(DILATIONS), C, 3 * C), jnp.float32) * 0.02
        Wproj = jax.random.normal(k2, (C, C), jnp.float32) * 0.02
        bproj = jnp.zeros((C,), jnp.float32)
        return {'x': x, 'Wqkv': Wqkv, 'Wproj': Wproj, 'bproj': bproj}
    _L2_attn_all = _L2_attn_setup()
    _L2_attn_in = {k: v for k, v in _L2_attn_all.items() if k in ('Wqkv', 'Wproj', 'bproj')}
    del _L2_attn_all

    def _L2_ffn_setup():
        import jax, jax.numpy as jnp
        import numpy as np
        B, T, D, H, E = (16, 1024, 64, 128, 8)
        key = jax.random.key(seed)
        ks = jax.random.split(key, 5)
        x = jax.random.normal(ks[0], (B, T, D), dtype=jnp.float32)
        gate_w = jax.random.normal(ks[1], (D, E), dtype=jnp.float32) * 0.02
        gate_b = jnp.zeros((E,), dtype=jnp.float32)
        W1 = jax.random.normal(ks[2], (E, D, H), dtype=jnp.float32) * 0.02
        b1 = jnp.zeros((E, H), dtype=jnp.float32)
        W2 = jax.random.normal(ks[3], (E, H, D), dtype=jnp.float32) * 0.02
        b2 = jnp.zeros((E, D), dtype=jnp.float32)
        return {'x': x, 'gate_w': gate_w, 'gate_b': gate_b, 'W1': W1, 'b1': b1, 'W2': W2, 'b2': b2}
    _L2_ffn_all = _L2_ffn_setup()
    _L2_ffn_in = {k: v for k, v in _L2_ffn_all.items() if k in ('gate_w', 'gate_b', 'W1', 'b1', 'W2', 'b2')}
    del _L2_ffn_all

    def _L3_attn_setup():
        import jax, jax.numpy as jnp
        import numpy as np
        T, N, D = (128, 256, 64)

        def _causal_attend(H, e):
            n = H.shape[1]
            m0 = jnp.full((n,), -jnp.inf, dtype=H.dtype)
            s0 = jnp.zeros((n,), dtype=H.dtype)
            num0 = jnp.zeros((n, H.shape[2]), dtype=H.dtype)

            def step(carry, inp):
                m, s, num = carry
                e_t, h_t = inp
                m_new = jnp.maximum(m, e_t)
                alpha = jnp.exp(m - m_new)
                p = jnp.exp(e_t - m_new)
                s_new = s * alpha + p
                num_new = num * alpha[:, None] + p[:, None] * h_t
                c_t = num_new / s_new[:, None]
                return ((m_new, s_new, num_new), c_t)
            _, C = jax.lax.scan(step, (m0, s0, num0), (e, H))
            return C
        key = jax.random.key(seed)
        k1, k2, k3, k4 = jax.random.split(key, 4)
        scale = 1.0 / np.sqrt(D)
        return {'H': jax.random.normal(k1, (T, N, D), dtype=jnp.float32), 'fc_w': jax.random.normal(k2, (D, D), dtype=jnp.float32) * scale, 'fc_b': jax.random.normal(k3, (D,), dtype=jnp.float32) * scale, 'score_w': jax.random.normal(k4, (D,), dtype=jnp.float32) * scale}
    _L3_attn_all = _L3_attn_setup()
    _L3_attn_in = {k: v for k, v in _L3_attn_all.items() if k in ('fc_w', 'fc_b', 'score_w')}
    del _L3_attn_all

    def _L3_ffn_setup():
        import jax, jax.numpy as jnp
        import numpy as np
        from jax import lax
        key = jax.random.key(seed)
        B, T, I, H = (16, 512, 64, 64)
        ks = jax.random.split(key, 13)
        s = 1.0 / np.sqrt(H)

        def w(k, shape):
            return jax.random.uniform(k, shape, jnp.float32, -s, s)
        return {'x': jax.random.normal(ks[0], (B, T, I), jnp.float32), 'U_i': w(ks[1], (I, H)), 'V_i': w(ks[2], (H, H)), 'b_i': w(ks[3], (H,)), 'U_f': w(ks[4], (I, H)), 'V_f': w(ks[5], (H, H)), 'b_f': w(ks[6], (H,)), 'U_c': w(ks[7], (I, H)), 'V_c': w(ks[8], (H, H)), 'b_c': w(ks[9], (H,)), 'U_o': w(ks[10], (I, H)), 'V_o': w(ks[11], (H, H)), 'b_o': w(ks[12], (H,))}
    _L3_ffn_all = _L3_ffn_setup()
    _L3_ffn_in = {k: v for k, v in _L3_ffn_all.items() if k in ('U_i', 'V_i', 'b_i', 'U_f', 'V_f', 'b_f', 'U_c', 'V_c', 'b_c', 'U_o', 'V_o', 'b_o')}
    del _L3_ffn_all
    return {'x': x, 'L0_conv_qkv_w': _L0_conv_in['qkv_w'], 'L0_conv_qkv_b': _L0_conv_in['qkv_b'], 'L0_conv_rpb': _L0_conv_in['rpb'], 'L0_conv_proj_w': _L0_conv_in['proj_w'], 'L0_conv_proj_b': _L0_conv_in['proj_b'], 'L0_conv_g1_w': _L0_conv_in['g1_w'], 'L0_conv_g1_b': _L0_conv_in['g1_b'], 'L0_conv_g2_w': _L0_conv_in['g2_w'], 'L0_conv_g2_b': _L0_conv_in['g2_b'], 'L0_conv_ln_g': _L0_conv_in['ln_g'], 'L0_conv_ln_b': _L0_conv_in['ln_b'], 'L1_conv_gamma': _L1_conv_in['gamma'], 'L1_conv_beta': _L1_conv_in['beta'], 'L1_conv_Wq': _L1_conv_in['Wq'], 'L1_conv_bq': _L1_conv_in['bq'], 'L1_conv_Wk': _L1_conv_in['Wk'], 'L1_conv_bk': _L1_conv_in['bk'], 'L1_conv_Wv': _L1_conv_in['Wv'], 'L1_conv_bv': _L1_conv_in['bv'], 'L1_conv_Wp': _L1_conv_in['Wp'], 'L1_conv_bp': _L1_conv_in['bp'], 'L2_attn_Wqkv': _L2_attn_in['Wqkv'], 'L2_attn_Wproj': _L2_attn_in['Wproj'], 'L2_attn_bproj': _L2_attn_in['bproj'], 'L2_ffn_gate_w': _L2_ffn_in['gate_w'], 'L2_ffn_gate_b': _L2_ffn_in['gate_b'], 'L2_ffn_W1': _L2_ffn_in['W1'], 'L2_ffn_b1': _L2_ffn_in['b1'], 'L2_ffn_W2': _L2_ffn_in['W2'], 'L2_ffn_b2': _L2_ffn_in['b2'], 'L3_attn_fc_w': _L3_attn_in['fc_w'], 'L3_attn_fc_b': _L3_attn_in['fc_b'], 'L3_attn_score_w': _L3_attn_in['score_w'], 'L3_ffn_U_i': _L3_ffn_in['U_i'], 'L3_ffn_V_i': _L3_ffn_in['V_i'], 'L3_ffn_b_i': _L3_ffn_in['b_i'], 'L3_ffn_U_f': _L3_ffn_in['U_f'], 'L3_ffn_V_f': _L3_ffn_in['V_f'], 'L3_ffn_b_f': _L3_ffn_in['b_f'], 'L3_ffn_U_c': _L3_ffn_in['U_c'], 'L3_ffn_V_c': _L3_ffn_in['V_c'], 'L3_ffn_b_c': _L3_ffn_in['b_c'], 'L3_ffn_U_o': _L3_ffn_in['U_o'], 'L3_ffn_V_o': _L3_ffn_in['V_o'], 'L3_ffn_b_o': _L3_ffn_in['b_o']}

def reference(x, L0_conv_qkv_w, L0_conv_qkv_b, L0_conv_rpb, L0_conv_proj_w, L0_conv_proj_b, L0_conv_g1_w, L0_conv_g1_b, L0_conv_g2_w, L0_conv_g2_b, L0_conv_ln_g, L0_conv_ln_b, L1_conv_gamma, L1_conv_beta, L1_conv_Wq, L1_conv_bq, L1_conv_Wk, L1_conv_bk, L1_conv_Wv, L1_conv_bv, L1_conv_Wp, L1_conv_bp, L2_attn_Wqkv, L2_attn_Wproj, L2_attn_bproj, L2_ffn_gate_w, L2_ffn_gate_b, L2_ffn_W1, L2_ffn_b1, L2_ffn_W2, L2_ffn_b2, L3_attn_fc_w, L3_attn_fc_b, L3_attn_score_w, L3_ffn_U_i, L3_ffn_V_i, L3_ffn_b_i, L3_ffn_U_f, L3_ffn_V_f, L3_ffn_b_f, L3_ffn_U_c, L3_ffn_V_c, L3_ffn_b_c, L3_ffn_U_o, L3_ffn_V_o, L3_ffn_b_o):
    import jax
    import jax.numpy as jnp

    def _L0_conv_ref(x, qkv_w, qkv_b, rpb, proj_w, proj_b, g1_w, g1_b, g2_w, g2_b, ln_g, ln_b):
        import jax, jax.numpy as jnp
        import numpy as np
        DIM, K, NH = (64, 7, 8)

        def _nbhd_idx(n, k):
            start = jnp.clip(jnp.arange(n) - k // 2, 0, n - k)
            idx = start[:, None] + jnp.arange(k)[None, :]
            bias = idx - jnp.arange(n)[:, None] + (k - 1)
            return (idx, bias)
        B, H, W, C = x.shape
        hd = C // NH
        scale = hd ** (-0.5)
        qkv = x @ qkv_w + qkv_b
        q, kk, v = jnp.split(qkv, 3, axis=-1)
        q = q.reshape(B, H, W, NH, hd) * scale
        kk = kk.reshape(B, H, W, NH, hd)
        v = v.reshape(B, H, W, NH, hd)
        ih, bh = _nbhd_idx(H, K)
        iw, bw = _nbhd_idx(W, K)
        kn = kk[:, ih][:, :, :, iw].transpose(0, 1, 3, 5, 2, 4, 6)
        vn = v[:, ih][:, :, :, iw].transpose(0, 1, 3, 5, 2, 4, 6)
        attn = jnp.einsum('bijnd,bijnpqd->bijnpq', q, kn)
        bias = rpb[:, bh][:, :, :, bw]
        bias = bias.transpose(1, 3, 0, 2, 4)
        attn = attn + bias[None]
        a = jax.nn.softmax(attn.reshape(B, H, W, NH, K * K), axis=-1)
        a = a.reshape(B, H, W, NH, K, K)
        out = jnp.einsum('bijnpq,bijnpqd->bijnd', a, vn).reshape(B, H, W, C)
        out = out @ proj_w + proj_b
        gate = jax.nn.sigmoid(jax.nn.relu(x @ g1_w + g1_b) @ g2_w + g2_b)
        y = x + out * gate
        mu = jnp.mean(y, axis=-1, keepdims=True)
        var = jnp.var(y, axis=-1, keepdims=True)
        return (y - mu) / jnp.sqrt(var + 1e-05) * ln_g + ln_b

    def _L1_conv_ref(x, gamma, beta, Wq, bq, Wk, bk, Wv, bv, Wp, bp):
        import jax, jax.numpy as jnp
        import numpy as np
        UNITS = 64
        GROUPS = 8
        EPS = 0.001

        def group_norm(x, gamma, beta, groups=GROUPS, eps=EPS):
            B, H, W, C = x.shape
            xg = x.reshape(B, H, W, groups, C // groups)
            mean = xg.mean(axis=(1, 2, 4), keepdims=True)
            var = xg.var(axis=(1, 2, 4), keepdims=True)
            xn = (xg - mean) * jax.lax.rsqrt(var + eps)
            xn = xn.reshape(B, H, W, C)
            return xn * gamma + beta
        B, H, W, C = x.shape
        scale = jnp.float32(C) ** (-0.5)
        xn = group_norm(x, gamma, beta)
        n = H * W
        xf = xn.reshape(B, n, C)
        q = xf @ Wq + bq
        k = xf @ Wk + bk
        v = xf @ Wv + bv
        attn = jnp.einsum('bnc,bmc->bnm', q, k) * scale
        attn = jax.nn.softmax(attn, axis=-1)
        out = jnp.einsum('bnm,bmc->bnc', attn, v)
        out = out @ Wp + bp
        return xn + out.reshape(B, H, W, C)

    def _L2_attn_ref(x, Wqkv, Wproj, bproj):
        import jax, jax.numpy as jnp
        import numpy as np
        KERNEL_SIZE = 3
        DILATIONS = (1, 2, 3)

        def _window(t, dilation, ksize):
            B, N, C = t.shape
            pad = dilation * (ksize - 1) // 2
            tp = jnp.pad(t, ((0, 0), (pad, pad), (0, 0)))
            idx = jnp.arange(N)[:, None] + jnp.arange(ksize)[None, :] * dilation
            return tp[:, idx, :]
        B, N, C = x.shape
        scale = C ** (-0.5)
        outs = []
        for i, d in enumerate(DILATIONS):
            qkv = x @ Wqkv[i]
            q, k, v = jnp.split(qkv, 3, axis=-1)
            kw = _window(k, d, KERNEL_SIZE)
            vw = _window(v, d, KERNEL_SIZE)
            logits = jnp.einsum('bnc,bnkc->bnk', q, kw) * scale
            attn = jax.nn.softmax(logits, axis=-1)
            outs.append(jnp.einsum('bnk,bnkc->bnc', attn, vw))
        combined = jnp.mean(jnp.stack(outs, axis=0), axis=0)
        return combined @ Wproj + bproj

    def _L2_ffn_ref(x, gate_w, gate_b, W1, b1, W2, b2):
        import jax, jax.numpy as jnp
        import numpy as np
        B, T, D, H, E = (16, 1024, 64, 128, 8)
        Bb, Tt, Dd = x.shape
        Ee = gate_w.shape[1]
        xf = x.reshape(-1, Dd)
        N = xf.shape[0]
        logits = xf @ gate_w + gate_b
        probs = jax.nn.softmax(logits, axis=-1)
        top2_vals, top2_idx = jax.lax.top_k(probs, 2)
        cw = jnp.zeros((N, Ee), dtype=xf.dtype).at[jnp.arange(N)[:, None], top2_idx].add(top2_vals)

        def step(acc, params):
            w1, bb1, w2, bb2, we = params
            h = jax.nn.gelu(xf @ w1 + bb1, approximate=False)
            y = h @ w2 + bb2
            return (acc + we[:, None] * y, None)
        out, _ = jax.lax.scan(step, jnp.zeros_like(xf), (W1, b1, W2, b2, cw.T))
        return out.reshape(Bb, Tt, Dd)

    def _L3_attn_ref(H, fc_w, fc_b, score_w):
        import jax, jax.numpy as jnp
        import numpy as np
        T, N, D = (128, 256, 64)

        def _causal_attend(H, e):
            n = H.shape[1]
            m0 = jnp.full((n,), -jnp.inf, dtype=H.dtype)
            s0 = jnp.zeros((n,), dtype=H.dtype)
            num0 = jnp.zeros((n, H.shape[2]), dtype=H.dtype)

            def step(carry, inp):
                m, s, num = carry
                e_t, h_t = inp
                m_new = jnp.maximum(m, e_t)
                alpha = jnp.exp(m - m_new)
                p = jnp.exp(e_t - m_new)
                s_new = s * alpha + p
                num_new = num * alpha[:, None] + p[:, None] * h_t
                c_t = num_new / s_new[:, None]
                return ((m_new, s_new, num_new), c_t)
            _, C = jax.lax.scan(step, (m0, s0, num0), (e, H))
            return C
        Q = jnp.tanh(jnp.einsum('tnd,ed->tne', H, fc_w) + fc_b)
        e = jnp.einsum('tne,e->tn', Q, score_w)
        return _causal_attend(H, e)

    def _L3_ffn_ref(x, U_i, V_i, b_i, U_f, V_f, b_f, U_c, V_c, b_c, U_o, V_o, b_o):
        import jax, jax.numpy as jnp
        import numpy as np
        from jax import lax
        B, T, _ = x.shape
        H = U_i.shape[1]
        xt = jnp.swapaxes(x, 0, 1)
        xi = xt @ U_i + b_i
        xf = xt @ U_f + b_f
        xg = xt @ U_c + b_c
        xo = xt @ U_o + b_o
        h0 = jnp.zeros((B, H), x.dtype)
        c0 = jnp.zeros((B, H), x.dtype)

        def step(carry, xs):
            h, c = carry
            xi_t, xf_t, xg_t, xo_t = xs
            i_t = jax.nn.sigmoid(xi_t + h @ V_i)
            f_t = jax.nn.sigmoid(xf_t + h @ V_f)
            g_t = jnp.tanh(xg_t + h @ V_c)
            o_t = jax.nn.sigmoid(xo_t + h @ V_o)
            c_new = h * c + i_t * g_t
            h_new = o_t * jnp.tanh(c_new)
            return ((h_new, c_new), h_new)
        (_, _), hs = lax.scan(step, (h0, c0), (xi, xf, xg, xo))
        return jnp.swapaxes(hs, 0, 1)

    def _gn(v, G=32, eps=1e-05):
        B_, H_, W_, C_ = v.shape
        g = v.reshape(B_, H_, W_, G, C_ // G)
        m = jnp.mean(g, axis=(1, 2, 4), keepdims=True)
        s = jnp.var(g, axis=(1, 2, 4), keepdims=True)
        return ((g - m) / jnp.sqrt(s + eps)).reshape(v.shape)

    def _ln_c(v, eps=1e-06):
        m = jnp.mean(v, axis=-1, keepdims=True)
        s = jnp.var(v, axis=-1, keepdims=True)
        return (v - m) / jnp.sqrt(s + eps)

    def _ln_t(v, eps=1e-05):
        m = jnp.mean(v, axis=-1, keepdims=True)
        s = jnp.var(v, axis=-1, keepdims=True)
        return (v - m) / jnp.sqrt(s + eps)

    def _to_tokens(v):
        B_, H_, W_, C_ = v.shape
        return v.reshape(B_, H_ * W_, C_)

    def _from_tokens(t, like):
        return t.reshape(like.shape)
    x = _L0_conv_ref(x, L0_conv_qkv_w, L0_conv_qkv_b, L0_conv_rpb, L0_conv_proj_w, L0_conv_proj_b, L0_conv_g1_w, L0_conv_g1_b, L0_conv_g2_w, L0_conv_g2_b, L0_conv_ln_g, L0_conv_ln_b)
    x = _L1_conv_ref(x, L1_conv_gamma, L1_conv_beta, L1_conv_Wq, L1_conv_bq, L1_conv_Wk, L1_conv_bk, L1_conv_Wv, L1_conv_bv, L1_conv_Wp, L1_conv_bp)
    t = _to_tokens(x)
    t = t + _L2_attn_ref(_ln_t(t), L2_attn_Wqkv, L2_attn_Wproj, L2_attn_bproj)
    t = t + _L2_ffn_ref(_ln_t(t), L2_ffn_gate_w, L2_ffn_gate_b, L2_ffn_W1, L2_ffn_b1, L2_ffn_W2, L2_ffn_b2)
    t = t + _L3_attn_ref(_ln_t(t), L3_attn_fc_w, L3_attn_fc_b, L3_attn_score_w)
    t = t + _L3_ffn_ref(_ln_t(t), L3_ffn_U_i, L3_ffn_V_i, L3_ffn_b_i, L3_ffn_U_f, L3_ffn_V_f, L3_ffn_b_f, L3_ffn_U_c, L3_ffn_V_c, L3_ffn_b_c, L3_ffn_U_o, L3_ffn_V_o, L3_ffn_b_o)
    x = _from_tokens(t, x)
    return x

_drawn_inputs = setup_inputs


def setup_inputs(seed=0):
    import zlib

    import numpy as np

    out = dict(_drawn_inputs(seed))
    spreads = {'L0_conv_qkv_b': (0.0, 0.1),
     'L0_conv_proj_b': (0.0, 0.1),
     'L0_conv_g1_b': (0.0, 0.8),
     'L0_conv_ln_g': (1.0, 0.2),
     'L0_conv_ln_b': (0.0, 0.1),
     'L1_conv_gamma': (1.0, 0.2),
     'L1_conv_beta': (0.0, 0.1),
     'L1_conv_bq': (0.0, 2.0),
     'L1_conv_bk': (0.0, 2.0),
     'L1_conv_bv': (0.0, 2.0),
     'L1_conv_bp': (0.0, 0.1),
     'L2_attn_bproj': (0.0, 0.1),
     'L2_ffn_gate_b': (0.0, 0.41),
     'L2_ffn_b1': (0.0, 0.8),
     'L2_ffn_b2': (0.0, 0.367)}
    factors = {'L0_conv_rpb': 8.0,
     'L1_conv_Wq': 64.0,
     'L1_conv_Wk': 28.022,
     'L1_conv_Wv': 45.665,
     'L1_conv_Wp': 64.0,
     'L2_attn_Wqkv': 6.589,
     'L2_attn_Wproj': 6.699,
     'L2_ffn_gate_w': 3.542,
     'L2_ffn_W1': 8.0,
     'L2_ffn_W2': 8.0,
     'L3_attn_fc_b': 7.685,
     'L3_ffn_U_i': 3.345,
     'L3_ffn_V_i': 8.0,
     'L3_ffn_b_i': 8.0,
     'L3_ffn_V_c': 6.923,
     'L3_ffn_b_c': 6.017,
     'L3_ffn_U_o': 3.282,
     'L3_ffn_V_o': 8.0,
     'L3_ffn_b_o': 8.0}
    for name, (base, spread) in spreads.items():
        noise = np.random.default_rng([zlib.crc32(name.encode()), seed]).standard_normal(out[name].shape)
        drawn = base * np.exp(spread * noise) if base else spread * noise
        out[name] = jnp.asarray(drawn.astype(out[name].dtype))
    for name, factor in factors.items():
        out[name] = (out[name] * factor).astype(out[name].dtype)
    return out
```

```python
from contextlib import ExitStack

import concourse.bass as bass
from concourse import mybir

F32 = mybir.dt.float32
BF16 = mybir.dt.bfloat16
F16 = mybir.dt.float16
U32 = mybir.dt.uint32
ALU = mybir.AluOpType
ACT = mybir.ActivationFunctionType
AX = mybir.AxisListType

P = 128
B, SIDE, C = 2, 16, 64
N = SIDE * SIDE
HALVES = N // P
HEADS, HD, K = 8, 8, 7
BAND = 11
KEYS = BAND * SIDE
KCH = KEYS // 2
KROW0 = (0, SIDE - BAND)
APAD, BPAD = 4, 9
AROWS, BCOLS = 2 * K - 1 + 2 * APAD, 2 * K - 1 + 2 * BPAD
E, HID = 8, 128
DIL = (1, 2, 3)
PADT = 3
CHUNK = 8
STEPS_IN_BODY = 2 * CHUNK
HSCALE = 32768.0
GATES = "gio"

CONST = dict(ident=P, mean=P, group=P, eighth=P, dup0=P, diff=P, heads=HEADS, iota=E, band=2 * KEYS, onehot=E * P)
W0 = dict(q=P, k=P, v=P, g1=32, g2=P, proj=P)
W1 = dict(q=P, k=P, v=P, p=P)
W2 = {f"{n}{d}": P for d in range(3) for n in "qkv"} | dict(proj=P)
W3 = dict(gate=E, b2=C, up=E * HID, down=E * C)
W4 = dict(fc=P, s0=P, s1=P)
W5 = {f"U{g}": P for g in GATES} | {f"V{g}": P for g in GATES} | {f"b{g}": P for g in GATES}
VEC = ["bq0", "bk0", "bv0", "bp0", "g1b", "g2b", "lng", "lnb", "gamma", "beta", "bq1", "bk1", "bv1", "bp1",
       "bp2", "fcb"] + [f"b1_{e}" for e in range(E)]
VECS = {n: 1 for n in VEC} | dict(gateb=E)


def width(columns):
    return sum(columns.values())


def cols(tile, columns, name):
    at = 0
    for n, w in columns.items():
        if n == name:
            return tile[:, at:at + w]
        at += w
    raise KeyError(name)


def build(nc, x, const, vec, rpb, w0, w1, w2, w3, w4, w5, out):
    with ExitStack() as ctx:
        def sb(name, shape, dt=F32):
            return ctx.enter_context(nc.sbuf_tensor(name, shape, dt))

        semaphores = {}

        def on(name):
            if name not in semaphores:
                semaphores[name] = ctx.enter_context(nc.semaphore("s_" + name))
            return semaphores[name]

        bank = [ctx.enter_context(nc.psum_tensor(f"bank{i}", [P, 512], F32)) for i in range(8)]

        xtm = sb("xtm", [P, HALVES, B, C])
        cst = sb("cst", [P, width(CONST)])
        vcs = sb("vcs", [P, width(VECS)])
        w0s, w1s, w2s = sb("w0s", [P, width(W0)]), sb("w1s", [P, width(W1)]), sb("w2s", [P, width(W2)])
        w3s, w4s, w5s = sb("w3s", [P, width(W3)]), sb("w4s", [P, width(W4)]), sb("w5s", [P, width(W5)])
        rpbj = sb("rpbj", [SIDE, HEADS, AROWS, SIDE])
        bias = sb("bias", [P, HALVES, HEADS, KEYS])

        def c(name):
            return cols(cst, CONST, name)

        def v(name):
            return cols(vcs, VECS, name)

        xf = sb("xf", [P, N])
        q0 = sb("q0", [P, N])
        km = sb("km", [P, HEADS, N])
        vch = sb("vch", [KCH, 2 * HALVES, P])
        g1 = sb("g1", [32, N])
        g2bh = sb("g2bh", [P, 1])
        gate = sb("gate", [P, N])
        gateh = sb("gateh", [P, N])
        sc = sb("sc", [P, 4, 2, KEYS])
        pr = sb("pr", [P, 4, 2, KEYS])
        mx = sb("mx", [P, 32])
        nmx = sb("nmx", [P, 32])
        sums = sb("sums", [P, 32])
        rsum = sb("rsum", [P, 32])
        pt = sb("pt", [KCH, 2, 4, P])
        otm = sb("otm", [P, 32, HD])
        of = sb("of", [P, N])
        pg = sb("pg", [P, N])
        y0 = sb("y0", [P, N])
        dif, sq, sd, rs = (sb(n, [P, N]) for n in ("dif", "sq", "sd", "rs"))
        epsc = sb("epsc", [P, 2])
        lno = sb("lno", [P, N])
        t0 = sb("t0", [P, N])
        st6, st2, gst, gtm = sb("st6", [P, 6]), sb("st2", [P, 2]), sb("gst", [P, 2]), sb("gtm", [P, 8])
        xn = sb("xn", [P, N])
        q1, k1 = sb("q1", [P, N]), sb("k1", [P, N])
        v1 = sb("v1", [P, HALVES, P])
        p1 = sb("p1", [P, 4, N])
        nm1, sm1, rm1 = sb("nm1", [P, 4]), sb("sm1", [P, 4]), sb("rm1", [P, 4])
        ns1 = sb("ns1", [P, 4])
        pn1 = sb("pn1", [P, 4, N])
        pt1 = sb("pt1", [P, B, HALVES, N])
        o1 = sb("o1", [P, N])
        t1 = sb("t1", [P, N])
        x2 = sb("x2", [P, N])
        q2 = sb("q2", [P, 3, N])
        kp, vp = sb("kp", [P, 3, N + 2 * PADT]), sb("vp", [P, 3, N + 2 * PADT])
        qk = sb("qk", [P, 3, 3, N])
        m2a, m2 = sb("m2a", [P, 3, N]), sb("m2", [P, 3, N])
        ls = sb("ls", [P, 3, 3, N])
        ew = ls
        wv = qk
        de, ra, nu, nua, ox = (sb(n, [P, 3, N]) for n in ("de", "ra", "nu", "nua", "ox"))
        oa, ob = sb("oa", [P, N]), sb("ob", [P, N])
        t2 = sb("t2", [P, N])
        x3 = sb("x3", [P, B, N])
        lg, lg2, eg, pg3, cw = (sb(n, [P, 4, E]) for n in ("lg", "lg2", "eg", "pg3", "cw"))
        mg, sg, rg = sb("mg", [P, 4]), sb("sg", [P, 4]), sb("rg", [P, 4])
        top, topi, topf = sb("top", [P, 4, E]), sb("topi", [P, 4, E], U32), sb("topf", [P, 4, 2])
        ca, cb = sb("ca", [P, 4, E]), sb("cb", [P, 4, E])
        cwp = sb("cwp", [P, 4, 3, E], BF16)
        cr1, cr2 = sb("cr1", [P, 4, E]), sb("cr2", [P, 4, E])
        idb = sb("idb", [P, P], BF16)
        oneh = sb("oneh", [3 * E, E * P], BF16)
        cwt = sb("cwt", [3 * E, B * N], BF16)
        cwf = sb("cwf", [E, B * N])
        hg = sb("hg", [P, 2, B * N])
        hw = sb("hw", [P, 2, B * N])
        t3 = sb("t3", [P, N])
        x4 = sb("x4", [P, N])
        qt4 = sb("qt4", [P, N])
        sdf = sb("sdf", [P, P])
        wsig = sb("wsig", [P, N])
        junk = sb("junk", [P, 1])
        cc = sb("cc", [P, N])
        cc2 = sb("cc2", [P, N])
        t4 = sb("t4", [P, N])
        x5 = sb("x5", [P, N + 3 * CHUNK])
        vparts = sb("vparts", [P, 3, 3, P], BF16)
        vsc, vr1, vr2 = (sb(n, [P, 3 * P]) for n in ("vsc", "vr1", "vr2"))
        ones = sb("ones", [P, CHUNK])
        gi, go, gos = sb("gi", [P, 1]), sb("go", [P, 2]), sb("gos", [P, 1])
        cell, hc = sb("cell", [P, 1]), sb("hc", [P, 1])
        ha, hb = sb("ha", [P, 1], F16), sb("hb", [P, 1], F16)
        hs = sb("hs", [P, N + STEPS_IN_BODY])
        ysum = sb("ysum", [P, N])
        ytm = sb("ytm", [P, HALVES, B, C])

        ident = c("ident")
        UNITS = [(b, qt, pair) for qt in range(HALVES) for b in range(B) for pair in range(HEADS // 2)]
        NU = len(UNITS)
        gt, tc = bank[6][:, 0:1], bank[7][:, 0:1]

        block = ctx.enter_context(nc.Block())

        def ocol(b, qt, h):
            return qt * P + b * C + h * HD

        @block.sync
        def _(sp):
            for h in range(HALVES):
                sp.dma_start(xtm[:, h], x[:, h * P:(h + 1) * P, :].rearrange("b p c -> p b c")).then_inc(on("x_in"), 16)
            sp.dma_start(cst[:], const).then_inc(on("const_in"), 16)
            for w, name, dram in ((w1s, "w1_in", w1), (w2s, "w2_in", w2), (w3s, "w3_in", w3), (w4s, "w4_in", w4),
                                  (w5s, "w5_in", w5)):
                sp.dma_start(w[:], dram).then_inc(on(name), 16)
            for h in range(HALVES):
                sp.wait_ge(on("y_tm"), h + 1)
                sp.dma_start(out[:, h * P:(h + 1) * P, :].rearrange("b p c -> p b c"), ytm[:, h]).then_inc(on("out"), 16)
            sp.wait_ge(on("out"), 16 * HALVES)

        @block.gpsimd
        def _(pool):
            for j in range(SIDE):
                pool.dma_start(rpbj[j:j + 1], rpb[None, :, :, SIDE - 1 - j:2 * SIDE - 1 - j]).then_inc(on("rpbj_in"), 16)
            pool.memset(kp[:], 0.0).then_inc(on("kpad_zero"), 1)
            pool.memset(vp[:], 0.0).then_inc(on("vpad_zero"), 1)
            pool.memset(x5[:], 0.0).then_inc(on("x5_zero"), 1)
            pool.memset(x3[:], 0.0).then_inc(on("x3_zero"), 1)
            pool.memset(ones[:], 1.0).then_inc(on("ones_set"), 1)
            pool.memset(epsc[:, 0:1], 1e-5).then_inc(on("eps_set"), 1)
            pool.memset(epsc[:, 1:2], 1e-3).then_inc(on("eps_set"), 1)
            for qt in range(HALVES):
                pool.wait_ge(on("bias_in%d" % qt), 16 * 8)
                if qt == 0:
                    pool.wait_ge(on("const_in"), 16)
                for h in range(HEADS):
                    pool.tensor_tensor(bias[:, qt, h], bias[:, qt, h], c("band")[:, qt * KEYS:(qt + 1) * KEYS],
                                       ALU.add).then_inc(on("bias_ready"), 1)
            pool.tensor_copy(idb[:], ident).then_inc(on("idb_ready"), 1)
            pool.tensor_copy(oneh[:], c("onehot")[0:3 * E]).then_inc(on("oneh_ready"), 1)
            pool.wait_ge(on("w5_in"), 16)
            vw = w5s[:, 3 * P:6 * P]
            flat = vparts[:].rearrange("p a g m -> p a (g m)")
            pool.tensor_scalar(vsc[:], vw, 1.0 / HSCALE, None, ALU.mult).then_inc(on("v_split"), 1)
            pool.wait_ge(on("v_split"), 1)
            pool.tensor_copy(flat[:, 0], vsc[:]).then_inc(on("v_split"), 1)
            pool.wait_ge(on("v_split"), 2)
            pool.tensor_tensor(vr1[:], vsc[:], flat[:, 0], ALU.subtract).then_inc(on("v_split"), 1)
            pool.wait_ge(on("v_split"), 3)
            pool.tensor_copy(flat[:, 1], vr1[:]).then_inc(on("v_split"), 1)
            pool.wait_ge(on("v_split"), 4)
            pool.tensor_tensor(vr2[:], vr1[:], flat[:, 1], ALU.subtract).then_inc(on("v_split"), 1)
            pool.wait_ge(on("v_split"), 5)
            pool.tensor_copy(flat[:, 2], vr2[:]).then_inc(on("v_parts"), 1)

        @block.scalar
        def _(act):
            act.dma_start(w0s[:], w0).then_inc(on("w0_in"), 16)
            act.dma_start(vcs[:], vec).then_inc(on("vec_in"), 16)
            act.wait_ge(on("rpbj_in"), 16 * SIDE)
            for i in range(SIDE):
                qt, r = i // 8, i % 8
                a0 = KROW0[qt] - i + K - 1 + APAD
                act.dma_start(bias[r * SIDE:(r + 1) * SIDE, qt].rearrange("j h (a k) -> j h a k", k=SIDE),
                              rpbj[:, :, a0:a0 + BAND, :]).then_inc(on("bias_in%d" % qt), 16)
            act.wait_ge(on("g1_mm"), 1)
            act.wait_ge(on("vec_in"), 16)
            act.activation(g1[:], bank[3][0:32, 0:N], ACT.Relu, bias=v("g1b")[0:32]).then_inc(on("g1_ready"), 1)
            act.wait_ge(on("g2_mm"), 1)
            act.wait_ge(on("g2bh"), 1)
            act.activation(gateh[:], bank[7][:, 0:N], ACT.Tanh, bias=g2bh[:], scale=0.5).then_inc(on("gateh"), 1)
            for u in range(NU):
                act.wait_ge(on("neg_max"), u + 1)
                if u >= 4:
                    act.wait_ge(on("p_turned"), u - 3)
                for h in range(2):
                    k = 2 * u + h
                    act.activation(pr[:, u % 4, h], sc[:, u % 4, h], ACT.Exp, bias=nmx[:, k:k + 1],
                                   accum_out=sums[:, k:k + 1]).then_inc(on("p_ready"), 1)

            def root(n, eps):
                act.wait_ge(on("var_mm"), n)
                act.wait_ge(on("eps_set"), 2)
                act.activation(sd[:], bank[1][:, 0:N], ACT.Sqrt, bias=epsc[:, eps:eps + 1]).then_inc(on("root"), 1)

            root(1, 0)
            act.wait_ge(on("gvar"), 1)
            act.activation(gtm[:, 2:3], gtm[:, 1:2], ACT.Sqrt, bias=epsc[:, 1:2]).then_inc(on("gsd"), 1)
            for u in range(4):
                act.wait_ge(on("neg_max1"), u + 1)
                act.activation(p1[:, u], bank[2 + u][:, 0:N], ACT.Exp, bias=nm1[:, u:u + 1], scale=C ** -0.5,
                               accum_out=sm1[:, u:u + 1]).then_inc(on("p1_ready"), 1)
            root(2, 0)
            act.wait_ge(on("kpad_zero"), 1)
            act.wait_ge(on("vpad_zero"), 1)
            for d in range(3):
                act.wait_ge(on("qkv2_mm"), 3 * d + 3)
                act.activation(kp[:, d, PADT:PADT + N], bank[2 * d][:, N:2 * N], ACT.Copy).then_inc(on("k2_ready"), 1)
                act.activation(vp[:, d, PADT:PADT + N], bank[2 * d + 1][:, 0:N], ACT.Copy).then_inc(on("v2_ready"), 1)
            for d in range(3):
                act.wait_ge(on("shifted"), d + 1)
                act.activation(ew[:, d], ls[:, d], ACT.Exp).then_inc(on("e2_ready"), 1)
            root(3, 0)
            act.wait_ge(on("lg2"), 1)
            act.activation(eg[:], lg2[:], ACT.Exp).then_inc(on("eg"), 1)
            for e in range(E):
                act.wait_ge(on("up_mm"), e + 1)
                if e >= 2:
                    act.wait_ge(on("weighted"), e - 1)
                act.activation(hg[:, e % 2], bank[e % 2][:], ACT.Gelu, bias=v(f"b1_{e}")).then_inc(on("gelu"), 1)
            root(4, 0)
            act.activation(junk[:], epsc[:, 0:1], ACT.Sigmoid).then_inc(on("table"), 1)
            act.wait_ge(on("fc_mm"), 1)
            act.activation(qt4[:], bank[2][:, 0:N], ACT.Tanh, bias=v("fcb")).then_inc(on("qt4"), 1)
            act.wait_ge(on("score_mm"), 1)
            act.activation(wsig[:], bank[3][:, 0:N], ACT.Sigmoid).then_inc(on("wsig"), 1)
            root(5, 0)

            with act.Fori(0, N, STEPS_IN_BODY) as base:
                for u in range(STEPS_IN_BODY):
                    t, pre, at = base + u, (u // CHUNK) * 3, u % CHUNK
                    act.wait_ge(on("g_pre"), t + 1)
                    act.activation(gt, bank[pre][:, at:at + 1], ACT.Tanh).then_inc(on("g_gate"), 1)
                    act.wait_ge(on("i_pre"), t + 1)
                    act.activation(gi[:], bank[pre + 1][:, at:at + 1], ACT.Sigmoid).then_inc(on("i_gate"), 1)
                    act.wait_ge(on("o_pre"), t + 1)
                    act.wait_ge(on("hc_ready"), t + 1)
                    act.activation(go[:, u % 2:u % 2 + 1], bank[pre + 2][:, at:at + 1], ACT.Sigmoid)\
                       .then_inc(on("o_gate"), 1)
                    act.wait_ge(on("i_gate"), t + 1)
                    act.activation(tc, gt, ACT.Tanh, scale=gi[:], bias=hc[:]).then_inc(on("tanh_c"), 1)

        @block.tensor
        def _(pe):
            mm = pe.matmul
            pe.wait_ge(on("x_in"), 16 * HALVES)
            pe.wait_ge(on("const_in"), 16)
            for h in range(HALVES):
                pe.transpose(bank[7][:, h * P:(h + 1) * P], xtm[:, h].rearrange("p b c -> p (b c)"), ident)\
                  .then_inc(on("x_turned"), 1)
            pe.wait_ge(on("w0_in"), 16)
            pe.wait_ge(on("xf"), 1)
            mm(bank[0][:, 0:N], cols(w0s, W0, "q"), xf[:], start=True, stop=True).then_inc(on("q0_mm"), 1)
            mm(bank[1][:, 0:N], cols(w0s, W0, "k"), xf[:], start=True, stop=True).then_inc(on("k0_mm"), 1)
            for qt in range(HALVES):
                for ch in range(2):
                    at = KROW0[qt] * SIDE + ch * KCH
                    mm(bank[2][0:KCH, (2 * qt + ch) * P:(2 * qt + ch + 1) * P], xf[:, at:at + KCH],
                       cols(w0s, W0, "v"), start=True, stop=True).then_inc(on("v0_mm"), 1)
            mm(bank[3][0:32, 0:N], cols(w0s, W0, "g1"), xf[:], start=True, stop=True).then_inc(on("g1_mm"), 1)
            pe.wait_ge(on("g1_ready"), 1)
            mm(bank[7][:, 0:N], cols(w0s, W0, "g2")[0:32], g1[:], start=True, stop=True).then_inc(on("g2_mm"), 1)

            def scores(u):
                b, qt, pair = UNITS[u]
                r, k0 = slice(b * C, (b + 1) * C), KROW0[qt] * SIDE
                if u >= 4:
                    pe.wait_ge(on("row_max"), 2 * (u - 3))
                mm(bank[u % 4][:, 0:2 * KEYS], q0[r, qt * P:(qt + 1) * P],
                   km[r, 2 * pair:2 * pair + 2, k0:k0 + KEYS], start=True, stop=True).then_inc(on("s_mm"), 1)

            def turn(u):
                pe.wait_ge(on("p_ready"), 2 * u + 2)
                if u >= 2:
                    pe.wait_ge(on("pt_ready"), u - 1)
                for h in range(2):
                    for ch in range(2):
                        m = pe.transpose(bank[4 + u % 2][0:KCH, (2 * h + ch) * P:(2 * h + ch + 1) * P],
                                         pr[:, u % 4, h, ch * KCH:(ch + 1) * KCH], ident)
                m.then_inc(on("p_turned"), 1)

            def values(u):
                b, qt, pair = UNITS[u]
                pe.wait_ge(on("pt_ready"), u + 1)
                for h in range(2):
                    o = ocol(b, qt, 2 * pair + h)
                    for ch in range(2):
                        col = b * C + (2 * pair + h) * HD
                        m = mm(bank[6][:, o:o + HD], pt[:, u % 2, 2 * h + ch], vch[:, 2 * qt + ch, col:col + HD],
                               start=(ch == 0), stop=(ch == 1))
                m.then_inc(on("pv_mm"), 1)

            pe.wait_ge(on("q0"), 1)
            pe.wait_ge(on("km"), HEADS)
            pe.wait_ge(on("vch"), 1)
            pe.wait_ge(on("g1_ready"), 1)
            for u in range(NU + 2):
                if u < NU:
                    scores(u)
                if 1 <= u <= NU:
                    turn(u - 1)
                if u >= 2:
                    values(u - 2)
            pe.wait_ge(on("otm"), 1)
            for h in range(HALVES):
                pe.transpose(bank[0][:, h * P:(h + 1) * P],
                             otm[:, h * 16:(h + 1) * 16].rearrange("p a d -> p (a d)"), ident).then_inc(on("o_turned"), 1)
            pe.wait_ge(on("of"), 1)
            mm(bank[1][:, 0:N], cols(w0s, W0, "proj"), of[:], start=True, stop=True).then_inc(on("proj0_mm"), 1)

            def norm(n, src):
                mm(bank[0][:, 0:N], c("mean"), src, start=True, stop=True).then_inc(on("mean_mm"), 1)
                pe.wait_ge(on("squares"), n)
                mm(bank[1][:, 0:N], c("mean"), sq[:], start=True, stop=True).then_inc(on("var_mm"), 1)

            pe.wait_ge(on("y0"), 1)
            norm(1, y0[:])
            pe.wait_ge(on("gst"), 1)
            mm(bank[2][:, 0:2], c("group"), gst[:], start=True, stop=True).then_inc(on("group_mm"), 1)
            pe.wait_ge(on("w1_in"), 16)
            pe.wait_ge(on("xn"), 1)
            mm(bank[0][:, 0:N], cols(w1s, W1, "q"), xn[:], start=True, stop=True).then_inc(on("q1_mm"), 1)
            mm(bank[1][:, 0:N], cols(w1s, W1, "k"), xn[:], start=True, stop=True).then_inc(on("k1_mm"), 1)
            for h in range(HALVES):
                m = mm(bank[6][:, h * P:(h + 1) * P], xn[:, h * P:(h + 1) * P], cols(w1s, W1, "v"),
                       start=True, stop=True)
            m.then_inc(on("v1_mm"), 1)
            pe.wait_ge(on("q1"), 1)
            pe.wait_ge(on("k1"), 1)
            for u in range(4):
                b, qt = u // 2, u % 2
                r = slice(b * C, (b + 1) * C)
                mm(bank[2 + u][:, 0:N], q1[r, qt * P:(qt + 1) * P], k1[r, :], start=True, stop=True)\
                    .then_inc(on("s1_mm"), 1)
            for u in range(4):
                b, qt = u // 2, u % 2
                pe.wait_ge(on("pn1"), u + 1)
                for ch in range(HALVES):
                    m = pe.transpose((bank[7] if b == 0 else bank[0])[:, ch * N + qt * P:ch * N + (qt + 1) * P],
                                     pn1[:, u, ch * P:(ch + 1) * P], ident)
                m.then_inc(on("p1_turned"), 1)
            pe.wait_ge(on("v1"), 1)
            for b in range(B):
                pe.wait_ge(on("pt1"), b + 1)
                for ch in range(HALVES):
                    m = mm(bank[1][b * C:(b + 1) * C, 0:N], v1[:, ch, b * C:(b + 1) * C], pt1[:, b, ch],
                           start=(ch == 0), stop=(ch == 1))
            m.then_inc(on("o1_mm"), 1)
            pe.wait_ge(on("o1"), 1)
            mm(bank[2][:, 0:N], cols(w1s, W1, "p"), o1[:], start=True, stop=True).then_inc(on("proj1_mm"), 1)
            pe.wait_ge(on("t1"), 1)
            norm(2, t1[:])

            pe.wait_ge(on("w2_in"), 16)
            pe.wait_ge(on("x2"), 1)
            for d in range(3):
                for n, dst in (("q", bank[2 * d][:, 0:N]), ("k", bank[2 * d][:, N:2 * N]), ("v", bank[2 * d + 1][:, 0:N])):
                    mm(dst, cols(w2s, W2, f"{n}{d}"), x2[:], start=True, stop=True).then_inc(on("qkv2_mm"), 1)
            for d in range(3):
                pe.wait_ge(on("qk"), d + 1)
                if d == 0:
                    pe.wait_ge(on("v2_ready"), 3)
                    pe.wait_ge(on("q2_ready"), 3)
                mm(bank[2 * d][:, 0:2 * N], c("eighth"), qk[:, d, 0:2].rearrange("p j n -> p (j n)"),
                   start=True, stop=True)
                mm(bank[2 * d + 1][:, 0:N], c("eighth"), qk[:, d, 2], start=True, stop=True).then_inc(on("logit_mm"), 1)
            pe.wait_ge(on("ob"), 1)
            mm(bank[6][:, 0:N], cols(w2s, W2, "proj"), ob[:], start=True, stop=True).then_inc(on("proj2_mm"), 1)
            pe.wait_ge(on("t2"), 1)
            norm(3, t2[:])

            pe.wait_ge(on("w3_in"), 16)
            pe.wait_ge(on("x3"), B)
            for h in range(HALVES):
                for b in range(B):
                    u = h * B + b
                    m = mm(bank[2][:, u * E:(u + 1) * E], x3[:, b, h * P:(h + 1) * P], cols(w3s, W3, "gate"),
                           start=True, stop=True)
            m.then_inc(on("gate_mm"), 1)

            def up(e):
                if e >= 2:
                    pe.wait_ge(on("gelu"), e - 1)
                mm(bank[e % 2][:], cols(w3s, W3, "up")[:, e * HID:(e + 1) * HID], x3[:].rearrange("p b n -> p (b n)"),
                   start=True, stop=True).then_inc(on("up_mm"), 1)

            up(0)
            up(1)
            pe.wait_ge(on("idb_ready"), 1)
            pe.wait_ge(on("cw_parts"), 3)
            cwb = bank[3][:].bitcast(BF16)
            for h in range(HALVES):
                for b in range(B):
                    u, at = h * B + b, b * N + h * P
                    pe.transpose(cwb[0:3 * E, at:at + P], cwp[:, u].rearrange("p a e -> p (a e)"), idb[:])
                    m = pe.transpose(bank[4][0:E, at:at + P], cw[:, u], ident)
            m.then_inc(on("cw_turned"), 1)
            pe.wait_ge(on("cwt"), 2)
            pe.wait_ge(on("oneh_ready"), 1)
            for b in range(B):
                mm(bank[7][b * C:(b + 1) * C, 0:N], cols(w3s, W3, "b2")[0:E], cwf[:, b * N:(b + 1) * N],
                   start=True, stop=False, skip_group_check=True)
            for e in range(E + 1):
                if e < E:
                    if e >= 2:
                        pe.wait_ge(on("weighted"), e - 1)
                    mm(bank[5 + e % 2][:], oneh[:, e * P:(e + 1) * P], cwt[:], start=True, stop=True)\
                        .then_inc(on("cw_mm"), 1)
                    if e + 2 < E:
                        up(e + 2)
                if e >= 1:
                    pe.wait_ge(on("weighted"), e)
                    for b in range(B):
                        m = mm(bank[7][b * C:(b + 1) * C, 0:N], cols(w3s, W3, "down")[:, (e - 1) * C:e * C],
                               hw[:, (e - 1) % 2, b * N:(b + 1) * N], start=False, stop=(e == E), skip_group_check=True)
                    m.then_inc(on("down_mm"), 1)
            pe.wait_ge(on("t3"), 1)
            norm(4, t3[:])

            pe.wait_ge(on("w4_in"), 16)
            pe.wait_ge(on("x4"), 1)
            mm(bank[2][:, 0:N], cols(w4s, W4, "fc"), x4[:], start=True, stop=True).then_inc(on("fc_mm"), 1)
            mm(bank[4][:, 0:N], c("dup0"), x4[:], start=True, stop=True)
            mm(bank[5][:, 0:N], c("diff"), x4[:], start=True, stop=True).then_inc(on("dup_mm"), 1)
            pe.wait_ge(on("sdf"), 1)
            pe.wait_ge(on("qt4"), 1)
            mm(bank[3][:, 0:N], sdf[:], qt4[:], start=True, stop=True).then_inc(on("score_mm"), 1)
            pe.wait_ge(on("t4"), 1)
            norm(5, t4[:])

            def x_part(parity, k, start):
                return mm(bank[3 * parity + k][:, 0:CHUNK], w5s[:, k * P:(k + 1) * P], x5[:, bass.ds(start, CHUNK)],
                          start=True, stop=False, skip_group_check=True)

            def b_part(parity, k):
                return mm(bank[3 * parity + k][:, 0:CHUNK], w5s[:, (6 + k) * P:(7 + k) * P], ones[:],
                          start=False, stop=False, skip_group_check=True)

            def recur(parity, k, at, part):
                for a in range(3):
                    m = mm(bank[3 * parity + k][:, at:at + 1], vparts[:, a, k], part, start=False, stop=False,
                           skip_group_check=True)
                return m

            pe.wait_ge(on("w5_in"), 16)
            pe.wait_ge(on("ones_set"), 1)
            pe.wait_ge(on("v_parts"), 1)
            pe.wait_ge(on("x5"), 1)
            for k in range(3):
                x_part(0, k, 0)
                b_part(0, k)
            with pe.Fori(0, N, STEPS_IN_BODY) as base:
                for u in range(STEPS_IN_BODY):
                    t, parity, at = base + u, u // CHUNK, u % CHUNK
                    pe.wait_ge(on("ha_ready"), t + 1)
                    for k in range(3):
                        recur(parity, k, at, ha[:])
                    pe.wait_ge(on("hb_ready"), t + 1)
                    recur(parity, 0, at, hb[:]).then_inc(on("g_pre"), 1)
                    recur(parity, 1, at, hb[:]).then_inc(on("i_pre"), 1)
                    recur(parity, 2, at, hb[:]).then_inc(on("o_pre"), 1)
                    if at < 3:
                        x_part(1 - parity, at, base + (parity + 1) * CHUNK)
                    elif at < 6:
                        b_part(1 - parity, at - 3)
            pe.wait_ge(on("ysum"), 1)
            for h in range(HALVES):
                pe.transpose(bank[h][:, 0:P], ysum[:, h * P:(h + 1) * P], ident).then_inc(on("y_turned"), 1)

        @block.vector
        def _(dve):
            tt, ts, stt = dve.tensor_tensor, dve.tensor_scalar, dve.scalar_tensor_tensor
            links = [0]

            def link(ins):
                links[0] += 1
                ins.then_inc(on("dve_link"), 1)
                dve.wait_ge(on("dve_link"), links[0])

            dve.wait_ge(on("x_turned"), HALVES)
            dve.tensor_copy(xf[:], bank[7][:, 0:N]).then_inc(on("xf"), 1)
            dve.wait_ge(on("vec_in"), 16)
            ts(g2bh[:], v("g2b"), 0.5, None, ALU.mult).then_inc(on("g2bh"), 1)
            dve.wait_ge(on("q0_mm"), 1)
            ts(q0[:], bank[0][:, 0:N], v("bq0"), HD ** -0.5, ALU.add, ALU.mult).then_inc(on("q0"), 1)
            dve.wait_ge(on("k0_mm"), 1)
            for h in range(HEADS):
                ts(km[:, h], bank[1][:, 0:N], v("bk0"), c("heads")[:, h:h + 1], ALU.add, ALU.mult).then_inc(on("km"), 1)
            dve.wait_ge(on("v0_mm"), 4)
            dve.tensor_copy(vch[:].rearrange("p a c -> p (a c)"), bank[2][0:KCH, :]).then_inc(on("vch"), 1)

            def row_max(u):
                b, qt, pair = UNITS[u]
                dve.wait_ge(on("s_mm"), u + 1)
                dve.wait_ge(on("bias_ready"), (qt + 1) * HEADS)
                if u >= 4:
                    dve.wait_ge(on("p_ready"), 2 * (u - 3))
                for h in range(2):
                    k = 2 * u + h
                    dve.tensor_tensor_reduce(sc[:, u % 4, h], bank[u % 4][:, h * KEYS:(h + 1) * KEYS],
                                             bias[:, qt, 2 * pair + h], 1.0, -3.0e38, ALU.add, ALU.max,
                                             mx[:, k:k + 1]).then_inc(on("row_max"), 1)
                dve.wait_ge(on("row_max"), 2 * u + 2)
                ts(nmx[:, 2 * u:2 * u + 2], mx[:, 2 * u:2 * u + 2], -1.0, None, ALU.mult).then_inc(on("neg_max"), 1)

            def pt_copy(u):
                dve.wait_ge(on("p_turned"), u + 1)
                if u >= 2:
                    dve.wait_ge(on("pv_mm"), u - 1)
                dve.tensor_copy(pt[:, u % 2].rearrange("p a c -> p (a c)"), bank[4 + u % 2][0:KCH, :])\
                   .then_inc(on("pt_ready"), 1)

            for u in range(NU + 2):
                if u < NU:
                    row_max(u)
                if u >= 2:
                    pt_copy(u - 2)
            dve.wait_ge(on("p_ready"), 2 * NU)
            link(dve.reciprocal(rsum[:], sums[:]))
            dve.wait_ge(on("pv_mm"), NU)
            tt(otm[:], bank[6][:, 0:32 * HD].rearrange("p (a d) -> p a d", d=HD),
               rsum[:][:, :, None].broadcast_to([P, 32, HD]), ALU.mult).then_inc(on("otm"), 1)
            dve.wait_ge(on("gateh"), 1)
            ts(gate[:], gateh[:], 0.5, 0.5, ALU.mult, ALU.add).then_inc(on("gate"), 1)
            dve.wait_ge(on("o_turned"), HALVES)
            ts(of[:], bank[0][:, 0:N], v("bv0"), None, ALU.add).then_inc(on("of"), 1)
            dve.wait_ge(on("proj0_mm"), 1)
            dve.wait_ge(on("gate"), 1)
            link(stt(out=pg[:], in0=bank[1][:, 0:N], scalar=v("bp0"), in1=gate[:], op0=ALU.add, op1=ALU.mult))
            tt(y0[:], pg[:], xf[:], ALU.add).then_inc(on("y0"), 1)

            def norm(n, src, dst, done):
                dve.wait_ge(on("mean_mm"), n)
                link(tt(dif[:], src, bank[0][:, 0:N], ALU.subtract))
                tt(sq[:], dif[:], dif[:], ALU.mult).then_inc(on("squares"), 1)
                dve.wait_ge(on("root"), n)
                link(dve.reciprocal(rs[:], sd[:]))
                if n == 3:
                    dve.wait_ge(on("x3_zero"), 1)
                    for b in range(B):
                        r = slice(b * C, (b + 1) * C)
                        tt(dst[r, b], dif[r, :], rs[r, :], ALU.mult).then_inc(on(done), 1)
                else:
                    tt(dst, dif[:], rs[:], ALU.mult).then_inc(on(done), 1)

            norm(1, y0[:], lno[:], "lno")
            dve.wait_ge(on("lno"), 1)
            ts(t0[:], lno[:], v("lng"), v("lnb"), ALU.mult, ALU.add).then_inc(on("t0"), 1)
            dve.wait_ge(on("t0"), 1)
            link(dve.bn_stats(st6[:], t0[:]))
            link(dve.bn_aggr(st2[:], st6[:]))
            dve.tensor_copy(gst[:, 0:1], st2[:, 0:1]).then_inc(on("gst_mean"), 1)
            stt(out=gst[:, 1:2], in0=st2[:, 0:1], scalar=st2[:, 0:1], in1=st2[:, 1:2], op0=ALU.mult, op1=ALU.add)\
                .then_inc(on("gst"), 1)
            dve.wait_ge(on("group_mm"), 1)
            link(dve.tensor_copy(gtm[:, 6:8], bank[2][:, 0:2]))
            link(tt(gtm[:, 0:1], gtm[:, 6:7], gtm[:, 6:7], ALU.mult))
            tt(gtm[:, 1:2], gtm[:, 7:8], gtm[:, 0:1], ALU.subtract).then_inc(on("gvar"), 1)
            dve.wait_ge(on("gsd"), 1)
            link(dve.reciprocal(gtm[:, 3:4], gtm[:, 2:3]))
            link(tt(gtm[:, 4:5], gtm[:, 3:4], v("gamma"), ALU.mult))
            link(ts(lno[:], t0[:], gtm[:, 6:7], gtm[:, 4:5], ALU.subtract, ALU.mult))
            ts(xn[:], lno[:], v("beta"), None, ALU.add).then_inc(on("xn"), 1)
            dve.wait_ge(on("q1_mm"), 1)
            ts(q1[:], bank[0][:, 0:N], v("bq1"), None, ALU.add).then_inc(on("q1"), 1)
            dve.wait_ge(on("k1_mm"), 1)
            ts(k1[:], bank[1][:, 0:N], v("bk1"), None, ALU.add).then_inc(on("k1"), 1)
            dve.wait_ge(on("v1_mm"), 1)
            dve.tensor_copy(v1[:].rearrange("p a c -> p (a c)"), bank[6][:, 0:N]).then_inc(on("v1"), 1)
            for u in range(4):
                dve.wait_ge(on("s1_mm"), u + 1)
                link(dve.tensor_reduce(ns1[:, u:u + 1], bank[2 + u][:, 0:N], AX.X, ALU.max))
                ts(nm1[:, u:u + 1], ns1[:, u:u + 1], -(C ** -0.5), None, ALU.mult).then_inc(on("neg_max1"), 1)
            for u in range(4):
                dve.wait_ge(on("p1_ready"), u + 1)
                link(dve.reciprocal(rm1[:, u:u + 1], sm1[:, u:u + 1]))
                ts(pn1[:, u], p1[:, u], rm1[:, u:u + 1], None, ALU.mult).then_inc(on("pn1"), 1)
            for b in range(B):
                dve.wait_ge(on("p1_turned"), 2 * b + 2)
                dve.tensor_copy(pt1[:, b].rearrange("p a c -> p (a c)"), (bank[7] if b == 0 else bank[0])[:])\
                   .then_inc(on("pt1"), 1)
            dve.wait_ge(on("o1_mm"), 1)
            ts(o1[:], bank[1][:, 0:N], v("bv1"), None, ALU.add).then_inc(on("o1"), 1)
            dve.wait_ge(on("proj1_mm"), 1)
            stt(out=t1[:], in0=bank[2][:, 0:N], scalar=v("bp1"), in1=xn[:], op0=ALU.add, op1=ALU.add)\
                .then_inc(on("t1"), 1)
            norm(2, t1[:], x2[:], "x2")

            for d in range(3):
                dve.wait_ge(on("qkv2_mm"), 3 * d + 3)
                dve.wait_ge(on("v2_ready"), d + 1)
                dve.tensor_copy(q2[:, d], bank[2 * d][:, 0:N]).then_inc(on("q2_ready"), 1)
                dve.wait_ge(on("q2_ready"), d + 1)
                for j in range(3):
                    s = PADT + (j - 1) * DIL[d]
                    m = tt(qk[:, d, j], q2[:, d], kp[:, d, s:s + N], ALU.mult)
                m.then_inc(on("qk"), 1)
            for d in range(3):
                l01 = bank[2 * d][:].rearrange("p (j n) -> p j n", j=2)
                l2 = bank[2 * d + 1][:, 0:N]
                dve.wait_ge(on("logit_mm"), d + 1)
                link(dve.tensor_copy(ls[:, d, 0:2], l01))
                link(tt(m2a[:, d], ls[:, d, 0], ls[:, d, 1], ALU.max))
                link(tt(m2[:, d], m2a[:, d], l2, ALU.max))
                tt(ls[:, d, 0], ls[:, d, 0], m2[:, d], ALU.subtract)
                tt(ls[:, d, 1], ls[:, d, 1], m2[:, d], ALU.subtract)
                tt(ls[:, d, 2], l2, m2[:, d], ALU.subtract).then_inc(on("shifted"), 1)
            for d in range(3):
                dve.wait_ge(on("e2_ready"), d + 1)
                tt(de[:, d], ew[:, d, 0], ew[:, d, 1], ALU.add).then_inc(on("de"), 1)
                dve.wait_ge(on("v2_ready"), 3)
                for j in range(3):
                    s = PADT + (j - 1) * DIL[d]
                    m = tt(wv[:, d, j], ew[:, d, j], vp[:, d, s:s + N], ALU.mult)
                m.then_inc(on("wv"), 1)
                dve.wait_ge(on("de"), d + 1)
                tt(m2[:, d], de[:, d], ew[:, d, 2], ALU.add).then_inc(on("den"), 1)
                dve.wait_ge(on("wv"), d + 1)
                tt(nua[:, d], wv[:, d, 0], wv[:, d, 1], ALU.add).then_inc(on("nua"), 1)
                dve.wait_ge(on("den"), d + 1)
                dve.reciprocal(ra[:, d], m2[:, d]).then_inc(on("ra"), 1)
                dve.wait_ge(on("nua"), d + 1)
                link(tt(nu[:, d], nua[:, d], wv[:, d, 2], ALU.add))
                link(tt(ox[:, d], nu[:, d], ra[:, d], ALU.mult))
            link(tt(oa[:], ox[:, 0], ox[:, 1], ALU.add))
            link(tt(ob[:], oa[:], ox[:, 2], ALU.add))
            ts(ob[:], ob[:], 1.0 / len(DIL), None, ALU.mult).then_inc(on("ob"), 1)
            dve.wait_ge(on("proj2_mm"), 1)
            stt(out=t2[:], in0=bank[6][:, 0:N], scalar=v("bp2"), in1=t1[:], op0=ALU.add, op1=ALU.add)\
                .then_inc(on("t2"), 1)
            norm(3, t2[:], x3[:], "x3")

            dve.wait_ge(on("gate_mm"), 1)
            link(tt(lg[:], bank[2][:, 0:4 * E].rearrange("p (u e) -> p u e", e=E),
               v("gateb")[:, None, :].broadcast_to([P, 4, E]), ALU.add))
            link(dve.tensor_reduce(mg[:], lg[:], AX.X, ALU.max))
            tt(lg2[:], lg[:], mg[:][:, :, None].broadcast_to([P, 4, E]), ALU.subtract).then_inc(on("lg2"), 1)
            dve.wait_ge(on("eg"), 1)
            link(dve.tensor_reduce(sg[:], eg[:], AX.X, ALU.add))
            link(dve.reciprocal(rg[:], sg[:]))
            link(tt(pg3[:], eg[:], rg[:][:, :, None].broadcast_to([P, 4, E]), ALU.mult))
            for u in range(4):
                dve.max(top[:, u], pg3[:, u]).then_inc(on("top"), 1)
            for u in range(4):
                dve.wait_ge(on("top"), u + 1)
                link(dve.max_index(topi[:, u], top[:, u], pg3[:, u]))
            link(dve.tensor_copy(topf[:], topi[:, :, 0:2]))
            for u in range(4):
                ts(ca[:, u], c("iota"), topf[:, u, 0:1], top[:, u, 0:1], ALU.is_equal, ALU.mult)
                m = ts(cb[:, u], c("iota"), topf[:, u, 1:2], top[:, u, 1:2], ALU.is_equal, ALU.mult)
            link(m)
            link(tt(cw[:], ca[:], cb[:], ALU.add))
            dve.tensor_copy(cwp[:, :, 0], cw[:]).then_inc(on("cw_parts"), 1)
            dve.wait_ge(on("cw_parts"), 1)
            link(tt(cr1[:], cw[:], cwp[:, :, 0], ALU.subtract))
            dve.tensor_copy(cwp[:, :, 1], cr1[:]).then_inc(on("cw_parts"), 1)
            dve.wait_ge(on("cw_parts"), 2)
            link(tt(cr2[:], cr1[:], cwp[:, :, 1], ALU.subtract))
            dve.tensor_copy(cwp[:, :, 2], cr2[:]).then_inc(on("cw_parts"), 1)
            dve.wait_ge(on("cw_turned"), 1)
            dve.tensor_copy(cwt[:], bank[3][:].bitcast(BF16)[0:3 * E, 0:B * N]).then_inc(on("cwt"), 1)
            dve.tensor_copy(cwf[:], bank[4][0:E, 0:B * N]).then_inc(on("cwt"), 1)
            for e in range(E):
                dve.wait_ge(on("gelu"), e + 1)
                dve.wait_ge(on("cw_mm"), e + 1)
                if e >= 2:
                    dve.wait_ge(on("down_mm"), e - 1)
                tt(hw[:, e % 2], hg[:, e % 2], bank[5 + e % 2][:], ALU.mult).then_inc(on("weighted"), 1)
            dve.wait_ge(on("down_mm"), E)
            tt(t3[:], bank[7][:, 0:N], t2[:], ALU.add).then_inc(on("t3"), 1)
            norm(4, t3[:], x4[:], "x4")

            dve.wait_ge(on("w4_in"), 16)
            tt(sdf[:], cols(w4s, W4, "s1"), cols(w4s, W4, "s0"), ALU.subtract).then_inc(on("sdf"), 1)
            dve.wait_ge(on("wsig"), 1)
            dve.wait_ge(on("dup_mm"), 1)
            tt(cc[:], bank[5][:, 0:N], wsig[:], ALU.mult).then_inc(on("cc"), 1)
            tt(cc2[:], bank[4][:, 0:N], t3[:], ALU.add).then_inc(on("cc"), 1)
            dve.wait_ge(on("cc"), 2)
            tt(t4[:], cc[:], cc2[:], ALU.add).then_inc(on("t4"), 1)
            dve.memset(hc[:], 0.0).then_inc(on("hc_ready"), 1)
            dve.memset(ha[:], 0.0).then_inc(on("ha_ready"), 1)
            dve.memset(hb[:], 0.0).then_inc(on("hb_ready"), 1)
            dve.wait_ge(on("x5_zero"), 1)
            norm(5, t4[:], x5[:, 0:N], "x5")

            with dve.Fori(0, N, STEPS_IN_BODY) as base:
                for u in range(STEPS_IN_BODY):
                    t, o = base + u, go[:, u % 2:u % 2 + 1]
                    dve.wait_ge(on("o_gate"), t + 1)
                    ts(gos[:], o, HSCALE, None, ALU.mult)
                    dve.wait_ge(on("tanh_c"), t + 1)
                    stt(out=ha[:], in0=tc, scalar=HSCALE, in1=o, op0=ALU.mult, op1=ALU.mult).then_inc(on("ha_ready"), 1)
                    stt(out=cell[:], in0=gt, scalar=gi[:], in1=hc[:], op0=ALU.mult, op1=ALU.add)
                    dve.wait_ge(on("ha_ready"), t + 2)
                    stt(out=hb[:], in0=tc, scalar=gos[:], in1=ha[:], op0=ALU.mult, op1=ALU.subtract)\
                        .then_inc(on("hb_ready"), 1)
                    tt(hs[:, bass.ds(t, 1)], tc, o, ALU.mult).then_inc(on("h_ready"), 1)
                    dve.wait_ge(on("h_ready"), t + 1)
                    tt(hc[:], hs[:, bass.ds(t, 1)], cell[:], ALU.mult).then_inc(on("hc_ready"), 1)
            dve.wait_ge(on("h_ready"), N)
            tt(ysum[:], hs[:, 0:N], t4[:], ALU.add).then_inc(on("ysum"), 1)
            for h in range(HALVES):
                dve.wait_ge(on("y_turned"), h + 1)
                dve.tensor_copy(ytm[:, h].rearrange("p b c -> p (b c)"), bank[h][:, 0:P]).then_inc(on("y_tm"), 1)


def constants(np):
    f = np.float32
    out = {}
    out["ident"] = np.eye(P, dtype=f)
    batch = np.arange(P) // C
    out["mean"] = (batch[:, None] == batch[None, :]).astype(f) / C
    groups = np.arange(P) // (C // 8)
    out["group"] = (groups[:, None] == groups[None, :]).astype(f) / (C // 8)
    out["eighth"] = (batch[:, None] == batch[None, :]).astype(f) * C ** -0.5
    src, dst = np.arange(P)[:, None], np.arange(P)[None, :]
    out["dup0"] = ((src < C) & (dst % C == src)).astype(f)
    out["diff"] = (dst >= C) * ((src == dst).astype(f) - (src == dst - C).astype(f))
    out["heads"] = ((np.arange(P) % C) // HD)[:, None] == np.arange(HEADS)[None, :]
    out["iota"] = np.tile(np.arange(E), (P, 1))
    start = np.clip(np.arange(SIDE) - K // 2, 0, SIDE - K)
    inside = (np.arange(SIDE)[None, :] >= start[:, None]) & (np.arange(SIDE)[None, :] < start[:, None] + K)
    band = np.zeros((2, 8, SIDE, BAND, SIDE), bool)
    for qt in range(2):
        rows = inside[8 * qt:8 * qt + 8, KROW0[qt]:KROW0[qt] + BAND]
        band[qt] = rows[:, None, :, None] & inside[None, :, None, :]
    band = np.where(band, 0.0, -1e30).reshape(2, P, KEYS)
    out["band"] = band.transpose(1, 0, 2).reshape(P, 2 * KEYS)
    one = np.zeros((P, E, P))
    for e in range(E):
        one[[e, E + e, 2 * E + e], e] = 1
    out["onehot"] = one.reshape(P, E * P)
    return np.concatenate([out[n].astype(f).reshape(P, w) for n, w in CONST.items()], axis=1)


def kernel(**inputs):
    import numpy as np
    import concourse.bacc as bacc
    from concourse.bass_utils import run_bass_kernel_spmd as run

    a = {n: np.asarray(x) for n, x in inputs.items()}

    def blocks(w):
        k, m = w.shape
        out = np.zeros((2 * k, 2 * m), w.dtype)
        out[:k, :m] = w
        out[k:, m:] = w
        return out

    def rows(w):
        return np.concatenate([w, np.zeros((P - w.shape[0], w.shape[1]), w.dtype)])

    def both(x):
        return rows(np.tile(x.reshape(-1, 1), (2, 1)))

    def pack(columns, parts):
        return np.ascontiguousarray(np.concatenate([parts[n] for n in columns], axis=1))

    L0 = {n[8:]: x for n, x in a.items() if n.startswith("L0_conv_")}
    L1 = {n[8:]: x for n, x in a.items() if n.startswith("L1_conv_")}
    F3 = {n[7:]: x for n, x in a.items() if n.startswith("L3_ffn_")}
    zero = np.zeros((C, C), np.float32)
    s = np.tile(a["L3_attn_score_w"].reshape(C, 1), (1, C))
    qkv = L0["qkv_w"]
    wqkv = a["L2_attn_Wqkv"]
    parts = {
        "w0": pack(W0, dict(q=blocks(qkv[:, :C]), k=blocks(qkv[:, C:2 * C]), v=blocks(qkv[:, 2 * C:]),
                            g1=blocks(L0["g1_w"]), g2=rows(blocks(np.tile(L0["g2_w"], (1, C)))),
                            proj=blocks(L0["proj_w"]))),
        "w1": pack(W1, dict(q=blocks(L1["Wq"]), k=blocks(L1["Wk"]), v=blocks(L1["Wv"]), p=blocks(L1["Wp"]))),
        "w2": pack(W2, {f"{n}{d}": blocks(wqkv[d][:, i * C:(i + 1) * C]) for d in range(3) for i, n in enumerate("qkv")}
                   | dict(proj=blocks(a["L2_attn_Wproj"]))),
        "w3": pack(W3, dict(gate=np.tile(a["L2_ffn_gate_w"], (2, 1)), b2=rows(a["L2_ffn_b2"]),
                            up=np.tile(a["L2_ffn_W1"].transpose(1, 0, 2).reshape(C, E * HID), (2, 1)),
                            down=a["L2_ffn_W2"].transpose(1, 0, 2).reshape(HID, E * C))),
        "w4": pack(W4, dict(fc=blocks(a["L3_attn_fc_w"].T),
                            s0=np.block([[zero, s], [zero, zero]]), s1=np.block([[zero, zero], [zero, s]]))),
    }
    lstm = {"g": "c", "i": "i", "o": "o"}
    parts["w5"] = pack(W5, {f"U{g}": blocks(F3[f"U_{n}"]) for g, n in lstm.items()}
                       | {f"V{g}": blocks(F3[f"V_{n}"]) for g, n in lstm.items()}
                       | {f"b{g}": rows(np.tile(F3[f"b_{n}"].reshape(1, C), (1, 2))) for g, n in lstm.items()})
    qb = L0["qkv_b"]
    vec = dict(bq0=qb[:C], bk0=qb[C:2 * C], bv0=qb[2 * C:], bp0=L0["proj_b"], g1b=L0["g1_b"],
               g2b=np.repeat(L0["g2_b"], C), lng=L0["ln_g"], lnb=L0["ln_b"], gamma=L1["gamma"], beta=L1["beta"],
               bq1=L1["bq"], bk1=L1["bk"], bv1=L1["bv"], bp1=L1["bp"], bp2=a["L2_attn_bproj"], fcb=a["L3_attn_fc_b"])
    vec = {n: both(x) for n, x in vec.items()} | {f"b1_{e}": a["L2_ffn_b1"][e].reshape(HID, 1) for e in range(E)}
    vec["gateb"] = np.tile(a["L2_ffn_gate_b"].reshape(1, E), (P, 1))
    parts["vec"] = pack(VECS, vec)
    parts["const"] = constants(np)
    parts["x"] = np.ascontiguousarray(a["x"].reshape(B, N, C))
    parts["rpb"] = np.pad(L0["rpb"], ((0, 0), (APAD, APAD), (BPAD, BPAD)))

    nc = bacc.Bacc("TRN2", target_bir_lowering=False, num_devices=1)
    order = ["x", "const", "vec", "rpb", "w0", "w1", "w2", "w3", "w4", "w5"]
    args = [nc.dram_tensor(f"in_{n}", parts[n].shape, mybir.dt.from_np(parts[n].dtype), kind="ExternalInput").ap()
            for n in order]
    args.append(nc.dram_tensor("out_y", (B, N, C), F32, kind="ExternalOutput").ap())
    build(nc, *args)
    r = run(nc, [{f"in_{n}": parts[n] for n in order}], core_ids=[0])
    return r.results[0]["out_y"].reshape(B, SIDE, SIDE, C)
```

```python
from contextlib import ExitStack

import concourse.bass as bass
from concourse import mybir

F32 = mybir.dt.float32
BF16 = mybir.dt.bfloat16
F16 = mybir.dt.float16
U32 = mybir.dt.uint32
ALU = mybir.AluOpType
ACT = mybir.ActivationFunctionType
AX = mybir.AxisListType

P = 128
B, SIDE, C = 2, 16, 64
N = SIDE * SIDE
HALVES = N // P
HEADS, HD, K = 8, 8, 7
BAND = 11
KEYS = BAND * SIDE
KCH = KEYS // 2
KROW0 = (0, SIDE - BAND)
APAD, BPAD = 4, 9
AROWS, BCOLS = 2 * K - 1 + 2 * APAD, 2 * K - 1 + 2 * BPAD
E, HID = 8, 128
DIL = (1, 2, 3)
PADT = 3
CHUNK = 8
STEPS_IN_BODY = 2 * CHUNK
HSCALE = 32768.0
GATES = "gio"

CONST = dict(ident=P, centre=P, means=B, heads=HEADS)
BANDS = dict(band=HALVES * KEYS)
LATER = dict(group=P, eighth=P, dup0=P, diff=P, iota=E, onehot=E * P)
W0 = dict(q=P, k=P, v=P, g1=32, g2=P, proj0=C, proj1=C)
W1 = dict(q=P, k=P, v=P, p=P)
W2 = {f"{n}{d}": P for d in range(3) for n in "qkv"} | dict(proj=P)
W3 = dict(gate=E, b2=C, up=E * HID, down=E * C)
W4 = dict(fc=P, s0=P, s1=P)
W5 = {f"U{g}": P for g in GATES} | {f"V{g}": P for g in GATES} | {f"b{g}": P for g in GATES}
VEC = ["bq0", "bk0", "bv0_0", "bv0_1", "bp0", "g1b", "g2b", "lng", "lnb", "gamma", "beta", "bq1", "bk1", "bv1", "bp1",
       "bp2", "fcb"] + [f"b1_{e}" for e in range(E)]
VECS = {n: 1 for n in VEC} | dict(gateb=E)


def width(columns):
    return sum(columns.values())


def cols(tile, columns, name):
    at = 0
    for n, w in columns.items():
        if n == name:
            return tile[:, at:at + w]
        at += w
    raise KeyError(name)


def build(nc, x, const, bands, later, vec, positions, w0, w1, w2, w3, w4, w5, out):
    with ExitStack() as ctx:
        def sb(name, shape, dt=F32):
            return ctx.enter_context(nc.sbuf_tensor(name, shape, dt))

        semaphores = {}

        def on(name):
            if name not in semaphores:
                semaphores[name] = ctx.enter_context(nc.semaphore("s_" + name))
            return semaphores[name]

        bank = [ctx.enter_context(nc.psum_tensor(f"bank{i}", [P, 512], F32)) for i in range(8)]

        xtm = sb("xtm", [P, HALVES, B, C])
        cst, bnd, ltr = sb("cst", [P, width(CONST)]), sb("bnd", [P, width(BANDS)]), sb("ltr", [P, width(LATER)])
        vcs = sb("vcs", [P, width(VECS)])
        w0s, w1s, w2s = sb("w0s", [P, width(W0)]), sb("w1s", [P, width(W1)]), sb("w2s", [P, width(W2)])
        w3s, w4s, w5s = sb("w3s", [P, width(W3)]), sb("w4s", [P, width(W4)]), sb("w5s", [P, width(W5)])
        bias = sb("bias", [P, HALVES, HEADS, KEYS])

        def c(name):
            for tile, columns in ((cst, CONST), (bnd, BANDS), (ltr, LATER)):
                if name in columns:
                    return cols(tile, columns, name)

        def v(name):
            return cols(vcs, VECS, name)

        xf = sb("xf", [P, N])
        q0 = sb("q0", [P, B, N])
        km = sb("km", [P, HEADS, N])
        k0 = sb("k0", [P, N])
        vch = sb("vch", [KCH, 2 * HALVES, B * HEADS, 32])
        g1 = sb("g1", [32, N])
        g2bh = sb("g2bh", [P, 1])
        gate = sb("gate", [P, N])
        gateh = sb("gateh", [P, N])
        sc = sb("sc", [P, 4, 2, KEYS])
        pr = sb("pr", [P, 4, 2, KEYS])
        mx = sb("mx", [P, 32])
        nmx = sb("nmx", [P, 32])
        sums = sb("sums", [P, 32])
        rsum = sb("rsum", [P, 32])
        pt = sb("pt", [KCH, 3, 4, P])
        of = sb("of", [P, 2, B * N])
        pg = sb("pg", [P, N])
        y0 = sb("y0", [P, N])
        sq, dif = sb("sq", [P, N]), sb("dif", [P, N])
        sd, rs = sb("sd", [P, HALVES, B]), sb("rs", [P, HALVES, B])
        rsw = sb("rsw", [P, HALVES, B, C])
        epsc = sb("epsc", [P, 2])
        lno = sb("lno", [P, N])
        t0 = sb("t0", [P, N])
        st6, st2, gst, gtm = sb("st6", [P, 6]), sb("st2", [P, 2]), sb("gst", [P, 2]), sb("gtm", [P, 8])
        xn = sb("xn", [P, N])
        q1, k1 = sb("q1", [P, N]), sb("k1", [P, N])
        v1 = sb("v1", [P, HALVES, P])
        p1 = sb("p1", [P, 4, N])
        nm1, sm1, rm1 = sb("nm1", [P, 4]), sb("sm1", [P, 4]), sb("rm1", [P, 4])
        ns1 = sb("ns1", [P, 4])
        pn1 = sb("pn1", [P, 4, N])
        pt1 = sb("pt1", [P, B, HALVES, N])
        o1 = sb("o1", [P, N])
        t1 = sb("t1", [P, N])
        x2 = sb("x2", [P, N])
        q2 = sb("q2", [P, 3, N])
        kp, vp = sb("kp", [P, 3, N + 2 * PADT]), sb("vp", [P, 3, N + 2 * PADT])
        qk = sb("qk", [P, 3, 3, N])
        m2a, m2 = sb("m2a", [P, 3, N]), sb("m2", [P, 3, N])
        ls = sb("ls", [P, 3, 3, N])
        ew = ls
        wv = qk
        de, ra, nu, nua, ox = (sb(n, [P, 3, N]) for n in ("de", "ra", "nu", "nua", "ox"))
        oa, ob = sb("oa", [P, N]), sb("ob", [P, N])
        t2 = sb("t2", [P, N])
        x3 = sb("x3", [P, B, N])
        lg, lg2, eg, pg3, cw = (sb(n, [P, 4, E]) for n in ("lg", "lg2", "eg", "pg3", "cw"))
        mg, sg, rg = sb("mg", [P, 4]), sb("sg", [P, 4]), sb("rg", [P, 4])
        top, topi, topf = sb("top", [P, 4, E]), sb("topi", [P, 4, E], U32), sb("topf", [P, 4, 2])
        ca, cb = sb("ca", [P, 4, E]), sb("cb", [P, 4, E])
        cwp = sb("cwp", [P, 4, 3, E], BF16)
        cr1, cr2 = sb("cr1", [P, 4, E]), sb("cr2", [P, 4, E])
        idb = sb("idb", [P, P], BF16)
        oneh = sb("oneh", [3 * E, E * P], BF16)
        cwt = sb("cwt", [3 * E, B * N], BF16)
        cwf = sb("cwf", [E, B * N])
        hg = sb("hg", [P, 2, B * N])
        hw = sb("hw", [P, 2, B * N])
        t3 = sb("t3", [P, N])
        x4 = sb("x4", [P, N])
        qt4 = sb("qt4", [P, N])
        sdf = sb("sdf", [P, P])
        wsig = sb("wsig", [P, N])
        junk = sb("junk", [P, 1])
        cc = sb("cc", [P, N])
        cc2 = sb("cc2", [P, N])
        t4 = sb("t4", [P, N])
        x5 = sb("x5", [P, N + 3 * CHUNK])
        vparts = sb("vparts", [P, 3, 3, P], BF16)
        vsc, vr1, vr2 = (sb(n, [P, 3 * P]) for n in ("vsc", "vr1", "vr2"))
        ones = sb("ones", [P, CHUNK])
        gi, go, gos = sb("gi", [P, 1]), sb("go", [P, 2]), sb("gos", [P, 1])
        cell, hc = sb("cell", [P, 1]), sb("hc", [P, 1])
        ha, hb = sb("ha", [P, 1], F16), sb("hb", [P, 1], F16)
        hs = sb("hs", [P, N + STEPS_IN_BODY])
        ysum = sb("ysum", [P, N])
        ytm = sb("ytm", [P, HALVES, B, C])

        ident = c("ident")
        dif_bank, var_bank, rs_bank = ({n: bank[3 * (n == 5) + i] for n in range(1, 6)} for i in (0, 1, 2))
        UNITS = [(b, qt, pair) for qt in range(HALVES) for b in range(B) for pair in range(HEADS // 2)]
        NU = len(UNITS)
        gt, tc = bank[6][:, 0:1], bank[7][:, 0:1]

        block = ctx.enter_context(nc.Block())

        @block.sync
        def _(sp):
            for b in range(B):
                sp.dma_start(xtm[:, :, b], x[b].rearrange("(h p) c -> p h c", h=HALVES)).then_inc(on("x_in"), 16)
            sp.dma_start(cst[:], const).then_inc(on("const_in"), 16)
            sp.dma_start(bnd[:], bands).then_inc(on("bands_in"), 16)
            sp.dma_start(bias[:, 1], positions[:, 1]).then_inc(on("bias_in1"), 16)
            for w, name, dram in ((ltr, "later_in", later), (w1s, "w1_in", w1), (w2s, "w2_in", w2), (w3s, "w3_in", w3),
                                  (w5s, "w5_in", w5), (w4s, "w4_in", w4)):
                sp.dma_start(w[:], dram).then_inc(on(name), 16)
            for h in range(HALVES):
                sp.wait_ge(on("y_tm"), h + 1)
                sp.dma_start(out[:, h * P:(h + 1) * P, :].rearrange("b p c -> p b c"), ytm[:, h]).then_inc(on("out"), 16)
            sp.wait_ge(on("out"), 16 * HALVES)

        @block.gpsimd
        def _(pool):
            pool.memset(q0[:], 0.0).then_inc(on("q0_zero"), 1)
            pool.memset(vch[:], 0.0).then_inc(on("vch_zero"), 1)
            pool.memset(kp[:], 0.0).then_inc(on("kpad_zero"), 1)
            pool.memset(vp[:], 0.0).then_inc(on("vpad_zero"), 1)
            pool.memset(x5[:], 0.0).then_inc(on("x5_zero"), 1)
            pool.memset(x3[:], 0.0).then_inc(on("x3_zero"), 1)
            pool.memset(ones[:], 1.0).then_inc(on("ones_set"), 1)
            pool.memset(epsc[:, 0:1], 1e-5).then_inc(on("eps_set"), 1)
            pool.memset(epsc[:, 1:2], 1e-3).then_inc(on("eps_set"), 1)
            for qt in range(HALVES):
                pool.wait_ge(on("bias_in%d" % qt), 16)
                if qt == 0:
                    pool.wait_ge(on("bands_in"), 16)
                for h in range(HEADS):
                    pool.tensor_tensor(bias[:, qt, h], bias[:, qt, h], c("band")[:, qt * KEYS:(qt + 1) * KEYS],
                                       ALU.add).then_inc(on("bias_ready"), 1)
            pool.wait_ge(on("const_in"), 16)
            pool.tensor_copy(idb[:], ident).then_inc(on("idb_ready"), 1)
            pool.wait_ge(on("later_in"), 16)
            pool.tensor_copy(oneh[:], c("onehot")[0:3 * E]).then_inc(on("oneh_ready"), 1)
            pool.wait_ge(on("w5_in"), 16)
            vw = w5s[:, 3 * P:6 * P]
            flat = vparts[:].rearrange("p a g m -> p a (g m)")
            pool.tensor_scalar(vsc[:], vw, 1.0 / HSCALE, None, ALU.mult).then_inc(on("v_split"), 1)
            pool.wait_ge(on("v_split"), 1)
            pool.tensor_copy(flat[:, 0], vsc[:]).then_inc(on("v_split"), 1)
            pool.wait_ge(on("v_split"), 2)
            pool.tensor_tensor(vr1[:], vsc[:], flat[:, 0], ALU.subtract).then_inc(on("v_split"), 1)
            pool.wait_ge(on("v_split"), 3)
            pool.tensor_copy(flat[:, 1], vr1[:]).then_inc(on("v_split"), 1)
            pool.wait_ge(on("v_split"), 4)
            pool.tensor_tensor(vr2[:], vr1[:], flat[:, 1], ALU.subtract).then_inc(on("v_split"), 1)
            pool.wait_ge(on("v_split"), 5)
            pool.tensor_copy(flat[:, 2], vr2[:]).then_inc(on("v_parts"), 1)

        @block.scalar
        def _(act):
            act.dma_start(w0s[:], w0).then_inc(on("w0_in"), 16)
            act.dma_start(vcs[:], vec).then_inc(on("vec_in"), 16)
            act.dma_start(bias[:, 0], positions[:, 0]).then_inc(on("bias_in0"), 16)
            act.wait_ge(on("g1_mm"), 1)
            act.wait_ge(on("vec_in"), 16)
            act.activation(g1[:], bank[3][0:32, 0:N], ACT.Relu, bias=v("g1b")[0:32]).then_inc(on("g1_ready"), 1)
            act.wait_ge(on("g2_mm"), 1)
            act.wait_ge(on("g2bh"), 1)
            act.activation(gateh[:], bank[7][:, 0:N], ACT.Tanh, bias=g2bh[:], scale=0.5).then_inc(on("gateh"), 1)
            act.wait_ge(on("vch_zero"), 1)
            act.wait_ge(on("v0_mm"), 4)
            act.activation(vch[:, :, :, 0:HD].rearrange("p a h d -> p (a h) d"),
                           bank[2][0:KCH, :].rearrange("p (a d) -> p a d", d=HD), ACT.Copy).then_inc(on("vch"), 1)

            def numerators(u):
                act.wait_ge(on("neg_max"), u + 1)
                if u >= 4:
                    act.wait_ge(on("p_turned"), u - 3)
                for h in range(2):
                    k = 2 * u + h
                    act.activation(pr[:, u % 4, h], sc[:, u % 4, h], ACT.Exp, bias=nmx[:, k:k + 1],
                                   accum_out=sums[:, k:k + 1]).then_inc(on("p_ready"), 1)

            def turned_copy(u):
                act.wait_ge(on("p_turned"), u + 1)
                if u >= 3:
                    act.wait_ge(on("pv_mm"), u - 2)
                act.activation(pt[:, u % 3].rearrange("p a c -> p (a c)"), bank[4 + u % 2][0:KCH, :], ACT.Copy)\
                   .then_inc(on("pt_ready"), 1)

            for u in range(NU + 2):
                if u < NU:
                    numerators(u)
                if u >= 2:
                    turned_copy(u - 2)

            def root(n):
                act.activation(junk[:], epsc[:, 0:1], ACT.Sqrt).then_inc(on("table"), 1)
                act.wait_ge(on("dif_mm"), n)
                act.activation(sq[:], dif_bank[n][:, 0:N], ACT.Square).then_inc(on("squares"), 1)
                act.wait_ge(on("var_mm"), n)
                act.wait_ge(on("eps_set"), 2)
                act.activation(sd[:].rearrange("p h b -> p (h b)"), var_bank[n][:, 0:HALVES * B], ACT.Sqrt,
                               bias=epsc[:, 0:1]).then_inc(on("root"), 1)

            root(1)
            act.wait_ge(on("gvar"), 1)
            act.activation(gtm[:, 2:3], gtm[:, 1:2], ACT.Sqrt, bias=epsc[:, 1:2]).then_inc(on("gsd"), 1)
            for u in range(4):
                act.wait_ge(on("neg_max1"), u + 1)
                act.activation(p1[:, u], bank[2 + u][:, 0:N], ACT.Exp, bias=nm1[:, u:u + 1], scale=C ** -0.5,
                               accum_out=sm1[:, u:u + 1]).then_inc(on("p1_ready"), 1)
            root(2)
            act.wait_ge(on("kpad_zero"), 1)
            act.wait_ge(on("vpad_zero"), 1)
            for d in range(3):
                act.wait_ge(on("qkv2_mm"), 3 * d + 3)
                act.activation(kp[:, d, PADT:PADT + N], bank[2 * d][:, N:2 * N], ACT.Copy).then_inc(on("k2_ready"), 1)
                act.activation(vp[:, d, PADT:PADT + N], bank[2 * d + 1][:, 0:N], ACT.Copy).then_inc(on("v2_ready"), 1)
            for d in range(3):
                act.wait_ge(on("shifted"), d + 1)
                act.activation(ew[:, d], ls[:, d], ACT.Exp).then_inc(on("e2_ready"), 1)
            root(3)
            act.wait_ge(on("lg2"), 1)
            act.activation(eg[:], lg2[:], ACT.Exp).then_inc(on("eg"), 1)
            for e in range(E):
                act.wait_ge(on("up_mm"), e + 1)
                if e >= 2:
                    act.wait_ge(on("weighted"), e - 1)
                act.activation(hg[:, e % 2], bank[e % 2][:], ACT.Gelu, bias=v(f"b1_{e}")).then_inc(on("gelu"), 1)
            root(4)
            act.activation(junk[:], epsc[:, 0:1], ACT.Sigmoid).then_inc(on("table"), 1)
            act.wait_ge(on("fc_mm"), 1)
            act.activation(qt4[:], bank[2][:, 0:N], ACT.Tanh, bias=v("fcb")).then_inc(on("qt4"), 1)
            act.wait_ge(on("score_mm"), 1)
            act.activation(wsig[:], bank[3][:, 0:N], ACT.Sigmoid).then_inc(on("wsig"), 1)
            root(5)
            act.activation(junk[:], epsc[:, 0:1], ACT.Sigmoid).then_inc(on("table"), 1)

            with act.Fori(0, N, STEPS_IN_BODY) as base:
                for u in range(STEPS_IN_BODY):
                    t, pre, at = base + u, (u // CHUNK) * 3, u % CHUNK
                    act.wait_ge(on("i_pre"), t + 1)
                    act.activation(gi[:], bank[pre + 1][:, at:at + 1], ACT.Sigmoid)
                    act.wait_ge(on("g_pre"), t + 1)
                    act.activation(gt, bank[pre][:, at:at + 1], ACT.Tanh).then_inc(on("gates"), 1)
                    act.wait_ge(on("o_pre"), t + 1)
                    act.wait_ge(on("hc_ready"), t + 1)
                    act.activation(go[:, u % 2:u % 2 + 1], bank[pre + 2][:, at:at + 1], ACT.Sigmoid)\
                       .then_inc(on("o_gate"), 1)
                    act.wait_ge(on("gates"), t + 1)
                    act.activation(tc, gt, ACT.Tanh, scale=gi[:], bias=hc[:]).then_inc(on("tanh_c"), 1)

        @block.tensor
        def _(pe):
            mm = pe.matmul
            pe.wait_ge(on("x_in"), 16 * HALVES)
            pe.wait_ge(on("const_in"), 16)
            for h in range(HALVES):
                pe.transpose(bank[7][:, h * P:(h + 1) * P], xtm[:, h].rearrange("p b c -> p (b c)"), ident)\
                  .then_inc(on("x_turned"), 1)
            pe.wait_ge(on("w0_in"), 16)
            pe.wait_ge(on("xf"), 1)
            mm(bank[0][:, 0:N], cols(w0s, W0, "q"), xf[:], start=True, stop=True).then_inc(on("q0_mm"), 1)
            mm(bank[1][:, 0:N], cols(w0s, W0, "k"), xf[:], start=True, stop=True).then_inc(on("k0_mm"), 1)
            for qt in range(HALVES):
                for ch in range(2):
                    at = KROW0[qt] * SIDE + ch * KCH
                    mm(bank[2][0:KCH, (2 * qt + ch) * P:(2 * qt + ch + 1) * P], xf[:, at:at + KCH],
                       cols(w0s, W0, "v"), start=True, stop=True).then_inc(on("v0_mm"), 1)
            mm(bank[3][0:32, 0:N], cols(w0s, W0, "g1"), xf[:], start=True, stop=True).then_inc(on("g1_mm"), 1)
            pe.wait_ge(on("g1_ready"), 1)
            mm(bank[7][:, 0:N], cols(w0s, W0, "g2")[0:32], g1[:], start=True, stop=True).then_inc(on("g2_mm"), 1)

            def scores(u):
                b, qt, pair = UNITS[u]
                at = KROW0[qt] * SIDE
                if u >= 4:
                    pe.wait_ge(on("row_max"), 2 * (u - 3))
                else:
                    pe.wait_ge(on("km"), 2 * pair + 2)
                mm(bank[u % 4][:, 0:2 * KEYS], q0[:, b, qt * P:(qt + 1) * P],
                   km[:, 2 * pair:2 * pair + 2, at:at + KEYS], start=True, stop=True).then_inc(on("s_mm"), 1)

            def turn(u):
                pe.wait_ge(on("normalised"), u + 1)
                if u >= 2:
                    pe.wait_ge(on("pt_ready"), u - 1)
                for h in range(2):
                    for ch in range(2):
                        m = pe.transpose(bank[4 + u % 2][0:KCH, (2 * h + ch) * P:(2 * h + ch + 1) * P],
                                         pr[:, u % 4, h, ch * KCH:(ch + 1) * KCH], ident)
                m.then_inc(on("p_turned"), 1)

            def values(u):
                b, qt, pair = UNITS[u]
                pe.wait_ge(on("pt_ready"), u + 1)
                for h in range(2):
                    g, j = divmod(2 * pair + h, 4)
                    for ch in range(2):
                        m = mm(bank[6 + g][32 * j:32 * (j + 1), (b * HALVES + qt) * P:(b * HALVES + qt + 1) * P],
                               vch[:, 2 * qt + ch, b * HEADS + 2 * pair + h], pt[:, u % 3, 2 * h + ch],
                               start=(ch == 0), stop=(ch == 1))
                m.then_inc(on("pv_mm"), 1)

            pe.wait_ge(on("q0"), B)
            pe.wait_ge(on("vch"), 1)
            pe.wait_ge(on("gateh"), 1)
            for u in range(NU + 4):
                if u < NU:
                    scores(u)
                if 2 <= u < NU + 2:
                    turn(u - 2)
                if u >= 4:
                    values(u - 4)
            for g in range(2):
                pe.wait_ge(on("of"), g + 1)
                for b in range(B):
                    m = mm(bank[1][b * C:(b + 1) * C, 0:N], cols(w0s, W0, f"proj{g}"), of[:, g, b * N:(b + 1) * N],
                           start=(g == 0), stop=(g == 1), skip_group_check=True)
            m.then_inc(on("proj0_mm"), 1)

            def norm(n, src):
                mm(dif_bank[n][:, 0:N], c("centre"), src, start=True, stop=True).then_inc(on("dif_mm"), 1)
                pe.wait_ge(on("squares"), n)
                for h in range(HALVES):
                    m = mm(var_bank[n][:, h * B:(h + 1) * B], sq[:, h * P:(h + 1) * P], c("means"), start=True, stop=True)
                m.then_inc(on("var_mm"), 1)
                pe.wait_ge(on("rs"), n)
                for h in range(HALVES):
                    m = pe.transpose(rs_bank[n][:, h * P:(h + 1) * P], rsw[:, h].rearrange("p b c -> p (b c)"), ident)
                m.then_inc(on("rs_mm"), 1)

            pe.wait_ge(on("y0"), 1)
            norm(1, y0[:])
            pe.wait_ge(on("later_in"), 16)
            pe.wait_ge(on("gst"), 1)
            mm(bank[2][:, 0:2], c("group"), gst[:], start=True, stop=True).then_inc(on("group_mm"), 1)
            pe.wait_ge(on("w1_in"), 16)
            pe.wait_ge(on("xn"), 1)
            mm(bank[0][:, 0:N], cols(w1s, W1, "q"), xn[:], start=True, stop=True).then_inc(on("q1_mm"), 1)
            mm(bank[1][:, 0:N], cols(w1s, W1, "k"), xn[:], start=True, stop=True).then_inc(on("k1_mm"), 1)
            for h in range(HALVES):
                m = mm(bank[6][:, h * P:(h + 1) * P], xn[:, h * P:(h + 1) * P], cols(w1s, W1, "v"),
                       start=True, stop=True)
            m.then_inc(on("v1_mm"), 1)
            pe.wait_ge(on("q1"), 1)
            pe.wait_ge(on("k1"), 1)
            for u in range(4):
                b, qt = u // 2, u % 2
                r = slice(b * C, (b + 1) * C)
                mm(bank[2 + u][:, 0:N], q1[r, qt * P:(qt + 1) * P], k1[r, :], start=True, stop=True)\
                    .then_inc(on("s1_mm"), 1)
            for u in range(4):
                b, qt = u // 2, u % 2
                pe.wait_ge(on("pn1"), u + 1)
                for ch in range(HALVES):
                    m = pe.transpose((bank[7] if b == 0 else bank[0])[:, ch * N + qt * P:ch * N + (qt + 1) * P],
                                     pn1[:, u, ch * P:(ch + 1) * P], ident)
                m.then_inc(on("p1_turned"), 1)
            pe.wait_ge(on("v1"), 1)
            for b in range(B):
                pe.wait_ge(on("pt1"), b + 1)
                for ch in range(HALVES):
                    m = mm(bank[1][b * C:(b + 1) * C, 0:N], v1[:, ch, b * C:(b + 1) * C], pt1[:, b, ch],
                           start=(ch == 0), stop=(ch == 1))
            m.then_inc(on("o1_mm"), 1)
            pe.wait_ge(on("o1"), 1)
            mm(bank[2][:, 0:N], cols(w1s, W1, "p"), o1[:], start=True, stop=True).then_inc(on("proj1_mm"), 1)
            pe.wait_ge(on("t1"), 1)
            norm(2, t1[:])

            pe.wait_ge(on("w2_in"), 16)
            pe.wait_ge(on("x2"), 1)
            for d in range(3):
                for n, dst in (("q", bank[2 * d][:, 0:N]), ("k", bank[2 * d][:, N:2 * N]), ("v", bank[2 * d + 1][:, 0:N])):
                    mm(dst, cols(w2s, W2, f"{n}{d}"), x2[:], start=True, stop=True).then_inc(on("qkv2_mm"), 1)
            for d in range(3):
                pe.wait_ge(on("qk"), d + 1)
                if d == 0:
                    pe.wait_ge(on("v2_ready"), 3)
                    pe.wait_ge(on("q2_ready"), 3)
                mm(bank[2 * d][:, 0:2 * N], c("eighth"), qk[:, d, 0:2].rearrange("p j n -> p (j n)"),
                   start=True, stop=True)
                mm(bank[2 * d + 1][:, 0:N], c("eighth"), qk[:, d, 2], start=True, stop=True).then_inc(on("logit_mm"), 1)
            pe.wait_ge(on("ob"), 1)
            mm(bank[6][:, 0:N], cols(w2s, W2, "proj"), ob[:], start=True, stop=True).then_inc(on("proj2_mm"), 1)
            pe.wait_ge(on("t2"), 1)
            norm(3, t2[:])

            pe.wait_ge(on("w3_in"), 16)
            pe.wait_ge(on("x3"), B)
            for h in range(HALVES):
                for b in range(B):
                    u = h * B + b
                    m = mm(bank[2][:, u * E:(u + 1) * E], x3[:, b, h * P:(h + 1) * P], cols(w3s, W3, "gate"),
                           start=True, stop=True)
            m.then_inc(on("gate_mm"), 1)

            def up(e):
                if e >= 2:
                    pe.wait_ge(on("gelu"), e - 1)
                mm(bank[e % 2][:], cols(w3s, W3, "up")[:, e * HID:(e + 1) * HID], x3[:].rearrange("p b n -> p (b n)"),
                   start=True, stop=True).then_inc(on("up_mm"), 1)

            up(0)
            up(1)
            pe.wait_ge(on("idb_ready"), 1)
            pe.wait_ge(on("cw_parts"), 3)
            cwb = bank[3][:].bitcast(BF16)
            for h in range(HALVES):
                for b in range(B):
                    u, at = h * B + b, b * N + h * P
                    pe.transpose(cwb[0:3 * E, at:at + P], cwp[:, u].rearrange("p a e -> p (a e)"), idb[:])
                    m = pe.transpose(bank[4][0:E, at:at + P], cw[:, u], ident)
            m.then_inc(on("cw_turned"), 1)
            pe.wait_ge(on("cwt"), 2)
            pe.wait_ge(on("oneh_ready"), 1)
            for b in range(B):
                mm(bank[7][b * C:(b + 1) * C, 0:N], cols(w3s, W3, "b2")[0:E], cwf[:, b * N:(b + 1) * N],
                   start=True, stop=False, skip_group_check=True)
            for e in range(E + 1):
                if e < E:
                    if e >= 2:
                        pe.wait_ge(on("weighted"), e - 1)
                    mm(bank[5 + e % 2][:], oneh[:, e * P:(e + 1) * P], cwt[:], start=True, stop=True)\
                        .then_inc(on("cw_mm"), 1)
                    if e + 2 < E:
                        up(e + 2)
                if e >= 1:
                    pe.wait_ge(on("weighted"), e)
                    for b in range(B):
                        m = mm(bank[7][b * C:(b + 1) * C, 0:N], cols(w3s, W3, "down")[:, (e - 1) * C:e * C],
                               hw[:, (e - 1) % 2, b * N:(b + 1) * N], start=False, stop=(e == E), skip_group_check=True)
                    m.then_inc(on("down_mm"), 1)
            pe.wait_ge(on("t3"), 1)
            norm(4, t3[:])

            pe.wait_ge(on("w4_in"), 16)
            pe.wait_ge(on("x4"), 1)
            mm(bank[2][:, 0:N], cols(w4s, W4, "fc"), x4[:], start=True, stop=True).then_inc(on("fc_mm"), 1)
            mm(bank[4][:, 0:N], c("dup0"), x4[:], start=True, stop=True)
            mm(bank[5][:, 0:N], c("diff"), x4[:], start=True, stop=True).then_inc(on("dup_mm"), 1)
            pe.wait_ge(on("sdf"), 1)
            pe.wait_ge(on("qt4"), 1)
            mm(bank[3][:, 0:N], sdf[:], qt4[:], start=True, stop=True).then_inc(on("score_mm"), 1)
            pe.wait_ge(on("t4"), 1)
            norm(5, t4[:])

            def b_part(parity, k):
                return mm(bank[3 * parity + k][:, 0:CHUNK], w5s[:, (6 + k) * P:(7 + k) * P], ones[:],
                          start=True, stop=False, skip_group_check=True)

            def x_part(parity, k, start):
                return mm(bank[3 * parity + k][:, 0:CHUNK], w5s[:, k * P:(k + 1) * P], x5[:, bass.ds(start, CHUNK)],
                          start=False, stop=False, skip_group_check=True)

            def recur(parity, k, at, part, terms):
                for a in range(terms):
                    m = mm(bank[3 * parity + k][:, at:at + 1], vparts[:, a, k], part, start=False, stop=False,
                           skip_group_check=True)
                return m

            pe.wait_ge(on("w5_in"), 16)
            pe.wait_ge(on("ones_set"), 1)
            for k in range(3):
                b_part(0, k)
            pe.wait_ge(on("v_parts"), 1)
            pe.wait_ge(on("x5"), 1)
            for k in (1, 0, 2):
                x_part(0, k, 0)
            with pe.Fori(0, N, STEPS_IN_BODY) as base:
                for u in range(STEPS_IN_BODY):
                    t, parity, at = base + u, u // CHUNK, u % CHUNK
                    pe.wait_ge(on("ha_ready"), t + 1)
                    for k in (1, 0, 2):
                        recur(parity, k, at, ha[:], 3)
                    pe.wait_ge(on("hb_ready"), t + 1)
                    recur(parity, 1, at, hb[:], 2).then_inc(on("i_pre"), 1)
                    recur(parity, 0, at, hb[:], 2).then_inc(on("g_pre"), 1)
                    recur(parity, 2, at, hb[:], 2).then_inc(on("o_pre"), 1)
                    if at < 3:
                        b_part(1 - parity, at)
                    elif at < 6:
                        x_part(1 - parity, at - 3, base + (parity + 1) * CHUNK)
            pe.wait_ge(on("ysum"), 1)
            for h in range(HALVES):
                pe.transpose(bank[h][:, 0:P], ysum[:, h * P:(h + 1) * P], ident).then_inc(on("y_turned"), 1)

        @block.vector
        def _(dve):
            tt, ts, stt = dve.tensor_tensor, dve.tensor_scalar, dve.scalar_tensor_tensor
            links = [0]

            def link(ins):
                links[0] += 1
                ins.then_inc(on("dve_link"), 1)
                dve.wait_ge(on("dve_link"), links[0])

            dve.wait_ge(on("x_turned"), HALVES)
            dve.tensor_copy(xf[:], bank[7][:, 0:N]).then_inc(on("xf"), 1)
            dve.wait_ge(on("vec_in"), 16)
            ts(g2bh[:], v("g2b"), 0.5, None, ALU.mult).then_inc(on("g2bh"), 1)
            dve.wait_ge(on("q0_mm"), 1)
            dve.wait_ge(on("q0_zero"), 1)
            for b in range(B):
                r = slice(b * C, (b + 1) * C)
                ts(q0[r, b], bank[0][r, 0:N], v("bq0")[r], HD ** -0.5, ALU.add, ALU.mult).then_inc(on("q0"), 1)
            dve.wait_ge(on("k0_mm"), 1)
            link(ts(k0[:], bank[1][:, 0:N], v("bk0"), None, ALU.add))
            for h in range(HEADS):
                ts(km[:, h], k0[:], c("heads")[:, h:h + 1], None, ALU.mult).then_inc(on("km"), 1)

            def row_max(u):
                b, qt, pair = UNITS[u]
                dve.wait_ge(on("s_mm"), u + 1)
                dve.wait_ge(on("bias_ready"), qt * HEADS + 2 * pair + 2)
                if u >= 4:
                    dve.wait_ge(on("p_ready"), 2 * (u - 3))
                for h in range(2):
                    k = 2 * u + h
                    dve.tensor_tensor_reduce(sc[:, u % 4, h], bank[u % 4][:, h * KEYS:(h + 1) * KEYS],
                                             bias[:, qt, 2 * pair + h], 1.0, -3.0e38, ALU.add, ALU.max,
                                             mx[:, k:k + 1]).then_inc(on("row_max"), 1)
                dve.wait_ge(on("row_max"), 2 * u + 2)
                ts(nmx[:, 2 * u:2 * u + 2], mx[:, 2 * u:2 * u + 2], -1.0, None, ALU.mult).then_inc(on("neg_max"), 1)

            def normalise(u):
                k = 2 * u
                dve.wait_ge(on("p_ready"), k + 2)
                link(dve.reciprocal(rsum[:, k:k + 2], sums[:, k:k + 2]))
                for h in range(2):
                    m = ts(pr[:, u % 4, h], pr[:, u % 4, h], rsum[:, k + h:k + h + 1], None, ALU.mult)
                m.then_inc(on("normalised"), 1)

            for u in range(NU + 1):
                if u < NU:
                    row_max(u)
                if u >= 1:
                    normalise(u - 1)
            dve.wait_ge(on("gateh"), 1)
            ts(gate[:], gateh[:], 0.5, 0.5, ALU.mult, ALU.add).then_inc(on("gate"), 1)
            dve.wait_ge(on("pv_mm"), NU)
            for g in range(2):
                ts(of[:, g], bank[6 + g][:], v(f"bv0_{g}"), None, ALU.add).then_inc(on("of"), 1)
            dve.wait_ge(on("proj0_mm"), 1)
            dve.wait_ge(on("gate"), 1)
            link(stt(out=pg[:], in0=bank[1][:, 0:N], scalar=v("bp0"), in1=gate[:], op0=ALU.add, op1=ALU.mult))
            tt(y0[:], pg[:], xf[:], ALU.add).then_inc(on("y0"), 1)

            def norm(n, dst, done):
                dve.wait_ge(on("squares"), n)
                dve.tensor_copy(dif[:], dif_bank[n][:, 0:N]).then_inc(on("dif"), 1)
                dve.wait_ge(on("root"), n)
                link(dve.reciprocal(rs[:], sd[:]))
                dve.tensor_copy(rsw[:], rs[:][:, :, :, None].broadcast_to([P, HALVES, B, C])).then_inc(on("rs"), 1)
                dve.wait_ge(on("rs_mm"), n)
                dve.wait_ge(on("dif"), n)
                if n == 3:
                    dve.wait_ge(on("x3_zero"), 1)
                    for b in range(B):
                        r = slice(b * C, (b + 1) * C)
                        tt(dst[r, b], dif[r, :], rs_bank[n][r, 0:N], ALU.mult).then_inc(on(done), 1)
                else:
                    tt(dst, dif[:], rs_bank[n][:, 0:N], ALU.mult).then_inc(on(done), 1)

            norm(1, lno[:], "lno")
            dve.wait_ge(on("lno"), 1)
            ts(t0[:], lno[:], v("lng"), v("lnb"), ALU.mult, ALU.add).then_inc(on("t0"), 1)
            dve.wait_ge(on("t0"), 1)
            link(dve.bn_stats(st6[:], t0[:]))
            link(dve.bn_aggr(st2[:], st6[:]))
            dve.tensor_copy(gst[:, 0:1], st2[:, 0:1]).then_inc(on("gst_mean"), 1)
            stt(out=gst[:, 1:2], in0=st2[:, 0:1], scalar=st2[:, 0:1], in1=st2[:, 1:2], op0=ALU.mult, op1=ALU.add)\
                .then_inc(on("gst"), 1)
            dve.wait_ge(on("group_mm"), 1)
            link(dve.tensor_copy(gtm[:, 6:8], bank[2][:, 0:2]))
            link(tt(gtm[:, 0:1], gtm[:, 6:7], gtm[:, 6:7], ALU.mult))
            tt(gtm[:, 1:2], gtm[:, 7:8], gtm[:, 0:1], ALU.subtract).then_inc(on("gvar"), 1)
            dve.wait_ge(on("gsd"), 1)
            link(dve.reciprocal(gtm[:, 3:4], gtm[:, 2:3]))
            link(tt(gtm[:, 4:5], gtm[:, 3:4], v("gamma"), ALU.mult))
            link(ts(lno[:], t0[:], gtm[:, 6:7], gtm[:, 4:5], ALU.subtract, ALU.mult))
            ts(xn[:], lno[:], v("beta"), None, ALU.add).then_inc(on("xn"), 1)
            dve.wait_ge(on("q1_mm"), 1)
            ts(q1[:], bank[0][:, 0:N], v("bq1"), None, ALU.add).then_inc(on("q1"), 1)
            dve.wait_ge(on("k1_mm"), 1)
            ts(k1[:], bank[1][:, 0:N], v("bk1"), None, ALU.add).then_inc(on("k1"), 1)
            dve.wait_ge(on("v1_mm"), 1)
            dve.tensor_copy(v1[:].rearrange("p a c -> p (a c)"), bank[6][:, 0:N]).then_inc(on("v1"), 1)
            for u in range(4):
                dve.wait_ge(on("s1_mm"), u + 1)
                link(dve.tensor_reduce(ns1[:, u:u + 1], bank[2 + u][:, 0:N], AX.X, ALU.max))
                ts(nm1[:, u:u + 1], ns1[:, u:u + 1], -(C ** -0.5), None, ALU.mult).then_inc(on("neg_max1"), 1)
            for u in range(4):
                dve.wait_ge(on("p1_ready"), u + 1)
                link(dve.reciprocal(rm1[:, u:u + 1], sm1[:, u:u + 1]))
                ts(pn1[:, u], p1[:, u], rm1[:, u:u + 1], None, ALU.mult).then_inc(on("pn1"), 1)
            for b in range(B):
                dve.wait_ge(on("p1_turned"), 2 * b + 2)
                dve.tensor_copy(pt1[:, b].rearrange("p a c -> p (a c)"), (bank[7] if b == 0 else bank[0])[:])\
                   .then_inc(on("pt1"), 1)
            dve.wait_ge(on("o1_mm"), 1)
            ts(o1[:], bank[1][:, 0:N], v("bv1"), None, ALU.add).then_inc(on("o1"), 1)
            dve.wait_ge(on("proj1_mm"), 1)
            stt(out=t1[:], in0=bank[2][:, 0:N], scalar=v("bp1"), in1=xn[:], op0=ALU.add, op1=ALU.add)\
                .then_inc(on("t1"), 1)
            norm(2, x2[:], "x2")

            for d in range(3):
                dve.wait_ge(on("qkv2_mm"), 3 * d + 3)
                dve.wait_ge(on("v2_ready"), d + 1)
                dve.tensor_copy(q2[:, d], bank[2 * d][:, 0:N]).then_inc(on("q2_ready"), 1)
                dve.wait_ge(on("q2_ready"), d + 1)
                for j in range(3):
                    s = PADT + (j - 1) * DIL[d]
                    m = tt(qk[:, d, j], q2[:, d], kp[:, d, s:s + N], ALU.mult)
                m.then_inc(on("qk"), 1)
            for d in range(3):
                l01 = bank[2 * d][:].rearrange("p (j n) -> p j n", j=2)
                l2 = bank[2 * d + 1][:, 0:N]
                dve.wait_ge(on("logit_mm"), d + 1)
                link(dve.tensor_copy(ls[:, d, 0:2], l01))
                link(tt(m2a[:, d], ls[:, d, 0], ls[:, d, 1], ALU.max))
                link(tt(m2[:, d], m2a[:, d], l2, ALU.max))
                tt(ls[:, d, 0], ls[:, d, 0], m2[:, d], ALU.subtract)
                tt(ls[:, d, 1], ls[:, d, 1], m2[:, d], ALU.subtract)
                tt(ls[:, d, 2], l2, m2[:, d], ALU.subtract).then_inc(on("shifted"), 1)
            for d in range(3):
                dve.wait_ge(on("e2_ready"), d + 1)
                tt(de[:, d], ew[:, d, 0], ew[:, d, 1], ALU.add).then_inc(on("de"), 1)
                dve.wait_ge(on("v2_ready"), 3)
                for j in range(3):
                    s = PADT + (j - 1) * DIL[d]
                    m = tt(wv[:, d, j], ew[:, d, j], vp[:, d, s:s + N], ALU.mult)
                m.then_inc(on("wv"), 1)
                dve.wait_ge(on("de"), d + 1)
                tt(m2[:, d], de[:, d], ew[:, d, 2], ALU.add).then_inc(on("den"), 1)
                dve.wait_ge(on("wv"), d + 1)
                tt(nua[:, d], wv[:, d, 0], wv[:, d, 1], ALU.add).then_inc(on("nua"), 1)
                dve.wait_ge(on("den"), d + 1)
                dve.reciprocal(ra[:, d], m2[:, d]).then_inc(on("ra"), 1)
                dve.wait_ge(on("nua"), d + 1)
                link(tt(nu[:, d], nua[:, d], wv[:, d, 2], ALU.add))
                link(tt(ox[:, d], nu[:, d], ra[:, d], ALU.mult))
            link(tt(oa[:], ox[:, 0], ox[:, 1], ALU.add))
            link(tt(ob[:], oa[:], ox[:, 2], ALU.add))
            ts(ob[:], ob[:], 1.0 / len(DIL), None, ALU.mult).then_inc(on("ob"), 1)
            dve.wait_ge(on("proj2_mm"), 1)
            stt(out=t2[:], in0=bank[6][:, 0:N], scalar=v("bp2"), in1=t1[:], op0=ALU.add, op1=ALU.add)\
                .then_inc(on("t2"), 1)
            norm(3, x3[:], "x3")

            dve.wait_ge(on("gate_mm"), 1)
            link(tt(lg[:], bank[2][:, 0:4 * E].rearrange("p (u e) -> p u e", e=E),
               v("gateb")[:, None, :].broadcast_to([P, 4, E]), ALU.add))
            link(dve.tensor_reduce(mg[:], lg[:], AX.X, ALU.max))
            tt(lg2[:], lg[:], mg[:][:, :, None].broadcast_to([P, 4, E]), ALU.subtract).then_inc(on("lg2"), 1)
            dve.wait_ge(on("eg"), 1)
            link(dve.tensor_reduce(sg[:], eg[:], AX.X, ALU.add))
            link(dve.reciprocal(rg[:], sg[:]))
            link(tt(pg3[:], eg[:], rg[:][:, :, None].broadcast_to([P, 4, E]), ALU.mult))
            for u in range(4):
                dve.max(top[:, u], pg3[:, u]).then_inc(on("top"), 1)
            for u in range(4):
                dve.wait_ge(on("top"), u + 1)
                link(dve.max_index(topi[:, u], top[:, u], pg3[:, u]))
            link(dve.tensor_copy(topf[:], topi[:, :, 0:2]))
            for u in range(4):
                ts(ca[:, u], c("iota"), topf[:, u, 0:1], top[:, u, 0:1], ALU.is_equal, ALU.mult)
                m = ts(cb[:, u], c("iota"), topf[:, u, 1:2], top[:, u, 1:2], ALU.is_equal, ALU.mult)
            link(m)
            link(tt(cw[:], ca[:], cb[:], ALU.add))
            dve.tensor_copy(cwp[:, :, 0], cw[:]).then_inc(on("cw_parts"), 1)
            dve.wait_ge(on("cw_parts"), 1)
            link(tt(cr1[:], cw[:], cwp[:, :, 0], ALU.subtract))
            dve.tensor_copy(cwp[:, :, 1], cr1[:]).then_inc(on("cw_parts"), 1)
            dve.wait_ge(on("cw_parts"), 2)
            link(tt(cr2[:], cr1[:], cwp[:, :, 1], ALU.subtract))
            dve.tensor_copy(cwp[:, :, 2], cr2[:]).then_inc(on("cw_parts"), 1)
            dve.wait_ge(on("cw_turned"), 1)
            dve.tensor_copy(cwt[:], bank[3][:].bitcast(BF16)[0:3 * E, 0:B * N]).then_inc(on("cwt"), 1)
            dve.tensor_copy(cwf[:], bank[4][0:E, 0:B * N]).then_inc(on("cwt"), 1)
            for e in range(E):
                dve.wait_ge(on("gelu"), e + 1)
                dve.wait_ge(on("cw_mm"), e + 1)
                if e >= 2:
                    dve.wait_ge(on("down_mm"), e - 1)
                tt(hw[:, e % 2], hg[:, e % 2], bank[5 + e % 2][:], ALU.mult).then_inc(on("weighted"), 1)
            dve.wait_ge(on("down_mm"), E)
            tt(t3[:], bank[7][:, 0:N], t2[:], ALU.add).then_inc(on("t3"), 1)
            norm(4, x4[:], "x4")

            dve.wait_ge(on("w4_in"), 16)
            tt(sdf[:], cols(w4s, W4, "s1"), cols(w4s, W4, "s0"), ALU.subtract).then_inc(on("sdf"), 1)
            dve.wait_ge(on("wsig"), 1)
            dve.wait_ge(on("dup_mm"), 1)
            tt(cc[:], bank[5][:, 0:N], wsig[:], ALU.mult).then_inc(on("cc"), 1)
            tt(cc2[:], bank[4][:, 0:N], t3[:], ALU.add).then_inc(on("cc"), 1)
            dve.wait_ge(on("cc"), 2)
            tt(t4[:], cc[:], cc2[:], ALU.add).then_inc(on("t4"), 1)
            dve.memset(hc[:], 0.0).then_inc(on("hc_ready"), 1)
            dve.memset(ha[:], 0.0).then_inc(on("ha_ready"), 1)
            dve.memset(hb[:], 0.0).then_inc(on("hb_ready"), 1)
            dve.wait_ge(on("x5_zero"), 1)
            norm(5, x5[:, 0:N], "x5")

            with dve.Fori(0, N, STEPS_IN_BODY) as base:
                for u in range(STEPS_IN_BODY):
                    t, o = base + u, go[:, u % 2:u % 2 + 1]
                    dve.wait_ge(on("o_gate"), t + 1)
                    ts(gos[:], o, HSCALE, None, ALU.mult)
                    dve.wait_ge(on("tanh_c"), t + 1)
                    stt(out=ha[:], in0=tc, scalar=HSCALE, in1=o, op0=ALU.mult, op1=ALU.mult).then_inc(on("ha_ready"), 1)
                    stt(out=cell[:], in0=gt, scalar=gi[:], in1=hc[:], op0=ALU.mult, op1=ALU.add)
                    dve.wait_ge(on("ha_ready"), t + 2)
                    stt(out=hb[:], in0=tc, scalar=gos[:], in1=ha[:], op0=ALU.mult, op1=ALU.subtract)\
                        .then_inc(on("hb_ready"), 1)
                    tt(hs[:, bass.ds(t, 1)], tc, o, ALU.mult).then_inc(on("h_ready"), 1)
                    dve.wait_ge(on("h_ready"), t + 1)
                    tt(hc[:], hs[:, bass.ds(t, 1)], cell[:], ALU.mult).then_inc(on("hc_ready"), 1)
            dve.wait_ge(on("h_ready"), N)
            tt(ysum[:], hs[:, 0:N], t4[:], ALU.add).then_inc(on("ysum"), 1)
            for h in range(HALVES):
                dve.wait_ge(on("y_turned"), h + 1)
                dve.tensor_copy(ytm[:, h].rearrange("p b c -> p (b c)"), bank[h][:, 0:P]).then_inc(on("y_tm"), 1)


def constants(np):
    f = np.float32
    out = {}
    out["ident"] = np.eye(P, dtype=f)
    batch = np.arange(P) // C
    same = (batch[:, None] == batch[None, :]).astype(f)
    out["centre"] = np.eye(P, dtype=f) - same / C
    out["means"] = (batch[:, None] == np.arange(B)[None, :]).astype(f) / C
    groups = np.arange(P) // (C // 8)
    out["group"] = (groups[:, None] == groups[None, :]).astype(f) / (C // 8)
    out["eighth"] = (batch[:, None] == batch[None, :]).astype(f) * C ** -0.5
    src, dst = np.arange(P)[:, None], np.arange(P)[None, :]
    out["dup0"] = ((src < C) & (dst % C == src)).astype(f)
    out["diff"] = (dst >= C) * ((src == dst).astype(f) - (src == dst - C).astype(f))
    out["heads"] = ((np.arange(P) % C) // HD)[:, None] == np.arange(HEADS)[None, :]
    out["iota"] = np.tile(np.arange(E), (P, 1))
    start = np.clip(np.arange(SIDE) - K // 2, 0, SIDE - K)
    inside = (np.arange(SIDE)[None, :] >= start[:, None]) & (np.arange(SIDE)[None, :] < start[:, None] + K)
    band = np.zeros((2, 8, SIDE, BAND, SIDE), bool)
    for qt in range(2):
        rows = inside[8 * qt:8 * qt + 8, KROW0[qt]:KROW0[qt] + BAND]
        band[qt] = rows[:, None, :, None] & inside[None, :, None, :]
    band = np.where(band, 0.0, -1e30).reshape(2, P, KEYS)
    out["band"] = band.transpose(1, 0, 2).reshape(P, 2 * KEYS)
    one = np.zeros((P, E, P))
    for e in range(E):
        one[[e, E + e, 2 * E + e], e] = 1
    out["onehot"] = one.reshape(P, E * P)
    return [np.concatenate([out[n].astype(f).reshape(P, w) for n, w in columns.items()], axis=1)
            for columns in (CONST, BANDS, LATER)]


def kernel(**inputs):
    import numpy as np
    import concourse.bacc as bacc
    from concourse.bass_utils import run_bass_kernel_spmd as run

    a = {n: np.asarray(x) for n, x in inputs.items()}

    def blocks(w):
        k, m = w.shape
        out = np.zeros((2 * k, 2 * m), w.dtype)
        out[:k, :m] = w
        out[k:, m:] = w
        return out

    def rows(w):
        return np.concatenate([w, np.zeros((P - w.shape[0], w.shape[1]), w.dtype)])

    def both(x):
        return rows(np.tile(x.reshape(-1, 1), (2, 1)))

    def spread(x):
        x = x.reshape(4, HD, -1)
        return np.pad(x, ((0, 0), (0, 32 - HD), (0, 0))).reshape(P, -1)

    def pack(columns, parts):
        return np.ascontiguousarray(np.concatenate([parts[n] for n in columns], axis=1))

    L0 = {n[8:]: x for n, x in a.items() if n.startswith("L0_conv_")}
    L1 = {n[8:]: x for n, x in a.items() if n.startswith("L1_conv_")}
    F3 = {n[7:]: x for n, x in a.items() if n.startswith("L3_ffn_")}
    zero = np.zeros((C, C), np.float32)
    s = np.tile(a["L3_attn_score_w"].reshape(C, 1), (1, C))
    qkv = L0["qkv_w"]
    wqkv = a["L2_attn_Wqkv"]
    parts = {
        "w0": pack(W0, dict(q=blocks(qkv[:, :C]), k=blocks(qkv[:, C:2 * C]), v=blocks(qkv[:, 2 * C:]),
                            g1=blocks(L0["g1_w"]), g2=rows(blocks(np.tile(L0["g2_w"], (1, C)))),
                            proj0=spread(L0["proj_w"][:P // 4]), proj1=spread(L0["proj_w"][P // 4:]))),
        "w1": pack(W1, dict(q=blocks(L1["Wq"]), k=blocks(L1["Wk"]), v=blocks(L1["Wv"]), p=blocks(L1["Wp"]))),
        "w2": pack(W2, {f"{n}{d}": blocks(wqkv[d][:, i * C:(i + 1) * C]) for d in range(3) for i, n in enumerate("qkv")}
                   | dict(proj=blocks(a["L2_attn_Wproj"]))),
        "w3": pack(W3, dict(gate=np.tile(a["L2_ffn_gate_w"], (2, 1)), b2=rows(a["L2_ffn_b2"]),
                            up=np.tile(a["L2_ffn_W1"].transpose(1, 0, 2).reshape(C, E * HID), (2, 1)),
                            down=a["L2_ffn_W2"].transpose(1, 0, 2).reshape(HID, E * C))),
        "w4": pack(W4, dict(fc=blocks(a["L3_attn_fc_w"].T),
                            s0=np.block([[zero, s], [zero, zero]]), s1=np.block([[zero, zero], [zero, s]]))),
    }
    lstm = {"g": "c", "i": "i", "o": "o"}
    parts["w5"] = pack(W5, {f"U{g}": blocks(F3[f"U_{n}"]) for g, n in lstm.items()}
                       | {f"V{g}": blocks(F3[f"V_{n}"]) for g, n in lstm.items()}
                       | {f"b{g}": rows(np.tile(F3[f"b_{n}"].reshape(1, C), (1, 2))) for g, n in lstm.items()})
    qb = L0["qkv_b"]
    vec = dict(bq0=qb[:C], bk0=qb[C:2 * C], bp0=L0["proj_b"], g1b=L0["g1_b"],
               g2b=np.repeat(L0["g2_b"], C), lng=L0["ln_g"], lnb=L0["ln_b"], gamma=L1["gamma"], beta=L1["beta"],
               bq1=L1["bq"], bk1=L1["bk"], bv1=L1["bv"], bp1=L1["bp"], bp2=a["L2_attn_bproj"], fcb=a["L3_attn_fc_b"])
    vec = {n: both(x) for n, x in vec.items()} | {f"b1_{e}": a["L2_ffn_b1"][e].reshape(HID, 1) for e in range(E)}
    vec |= {f"bv0_{g}": spread(qb[2 * C + g * C // 2:2 * C + (g + 1) * C // 2]) for g in range(2)}
    vec["gateb"] = np.tile(a["L2_ffn_gate_b"].reshape(1, E), (P, 1))
    parts["vec"] = pack(VECS, vec)
    parts["const"], parts["bands"], parts["later"] = constants(np)
    parts["x"] = np.ascontiguousarray(a["x"].reshape(B, N, C))
    rpb = np.pad(L0["rpb"], ((0, 0), (APAD, APAD), (BPAD, BPAD)))
    tiles = []
    for i in range(SIDE):
        a0, j0 = KROW0[i * HALVES // SIDE] - i + K - 1 + APAD, SIDE - 1
        tiles.append(np.stack([rpb[:, a0:a0 + BAND, j0 - j:j0 - j + SIDE].reshape(HEADS, KEYS) for j in range(SIDE)]))
    parts["positions"] = np.ascontiguousarray(np.stack(tiles).reshape(HALVES, P, HEADS, KEYS).transpose(1, 0, 2, 3))

    nc = bacc.Bacc("TRN2", target_bir_lowering=False, num_devices=1)
    order = ["x", "const", "bands", "later", "vec", "positions", "w0", "w1", "w2", "w3", "w4", "w5"]
    args = [nc.dram_tensor(f"in_{n}", parts[n].shape, mybir.dt.from_np(parts[n].dtype), kind="ExternalInput").ap()
            for n in order]
    args.append(nc.dram_tensor("out_y", (B, N, C), F32, kind="ExternalOutput").ap())
    build(nc, *args)
    r = run(nc, [{f"in_{n}": parts[n] for n in order}], core_ids=[0])
    return r.results[0]["out_y"].reshape(B, SIDE, SIDE, C)
```

```python
from contextlib import ExitStack

import concourse.bass as bass
from concourse import mybir

F32 = mybir.dt.float32
BF16 = mybir.dt.bfloat16
F16 = mybir.dt.float16
U32 = mybir.dt.uint32
ALU = mybir.AluOpType
ACT = mybir.ActivationFunctionType
AX = mybir.AxisListType

P = 128
B, SIDE, C = 2, 16, 64
N = SIDE * SIDE
HALVES = N // P
HEADS, HD, K = 8, 8, 7
BAND = 11
KEYS = BAND * SIDE
KCH = KEYS // 2
KROW0 = (0, SIDE - BAND)
APAD, BPAD = 4, 9
AROWS, BCOLS = 2 * K - 1 + 2 * APAD, 2 * K - 1 + 2 * BPAD
E, HID = 8, 128
DIL = (1, 2, 3)
UP_FIRST = 5
PADT = 3
CHUNK = 8
STEPS_IN_BODY = 2 * CHUNK
HSCALE = 256.0
GATES = "gio"

CONST = dict(ident=P, centre=P, means=B, heads=HEADS)
BANDS = dict(band=HALVES * KEYS)
LATER = dict(group=P, eighths=B, dup0=P, diff=P, iota=E, onehot=E * P)
W0 = dict(q=P, k=P, v=P, g1=32, g2=P, proj0=C, proj1=C)
W1 = dict(q=P, k=P, v=P, p=P)
W2 = {f"{n}{d}": P for d in range(3) for n in "qkv"} | dict(proj=P)
W3 = dict(gate=E, b2=C, up=E * HID, down=E * C)
W4 = dict(fc=P, s0=P, s1=P)
W5 = {f"U{g}": P for g in GATES} | {f"V{g}": P for g in GATES} | {f"b{g}": P for g in GATES}
VEC = ["bq0", "bk0", "bv0_0", "bv0_1", "bp0", "g1b", "g2b", "lng", "lnb", "gamma", "beta", "bq1", "bk1", "bv1", "bp1",
       "bp2", "fcb"] + [f"b1_{e}" for e in range(E)]
VECS = {n: 1 for n in VEC} | dict(gateb=E)


def width(columns):
    return sum(columns.values())


def cols(tile, columns, name):
    at = 0
    for n, w in columns.items():
        if n == name:
            return tile[:, at:at + w]
        at += w
    raise KeyError(name)


def build(nc, x, const, bands, later, vec, positions, w0, w1, w2, w3, w4, w5, out):
    with ExitStack() as ctx:
        def sb(name, shape, dt=F32):
            return ctx.enter_context(nc.sbuf_tensor(name, shape, dt))

        semaphores = {}

        def on(name):
            if name not in semaphores:
                semaphores[name] = ctx.enter_context(nc.semaphore("s_" + name))
            return semaphores[name]

        bank = [ctx.enter_context(nc.psum_tensor(f"bank{i}", [P, 512], F32)) for i in range(8)]

        xtm = sb("xtm", [P, HALVES, B, C])
        cst, bnd, ltr = sb("cst", [P, width(CONST)]), sb("bnd", [P, width(BANDS)]), sb("ltr", [P, width(LATER)])
        vcs = sb("vcs", [P, width(VECS)])
        w0s, w1s, w2s = sb("w0s", [P, width(W0)]), sb("w1s", [P, width(W1)]), sb("w2s", [P, width(W2)])
        w3s, w4s, w5s = sb("w3s", [P, width(W3)]), sb("w4s", [P, width(W4)]), sb("w5s", [P, width(W5)])
        bias = sb("bias", [P, HALVES, HEADS, KEYS])

        def c(name):
            for tile, columns in ((cst, CONST), (bnd, BANDS), (ltr, LATER)):
                if name in columns:
                    return cols(tile, columns, name)

        def v(name):
            return cols(vcs, VECS, name)

        xf = sb("xf", [P, N])
        q0 = sb("q0", [P, B, N])
        km = sb("km", [P, HEADS, N])
        k0 = sb("k0", [P, N])
        vch = sb("vch", [KCH, 2 * HALVES, B * HEADS, 32])
        g1 = sb("g1", [32, N])
        g2bh = sb("g2bh", [P, 1])
        gate = sb("gate", [P, N])
        gateh = sb("gateh", [P, N])
        sc = sb("sc", [P, 4, 2, KEYS])
        pr = sb("pr", [P, 5, 2, KEYS])
        nmx = sb("nmx", [P, 32])
        sums = sb("sums", [P, 32])
        rsum = sb("rsum", [P, 32])
        pt = sb("pt", [KCH, 3, 4, P])
        of = sb("of", [P, 2, B * N])
        pg = sb("pg", [P, N])
        y0 = sb("y0", [P, N])
        sq, dif = sb("sq", [P, N]), sb("dif", [P, N])
        sd, rs = sb("sd", [P, HALVES, B]), sb("rs", [P, HALVES, B])
        rsw = sb("rsw", [P, HALVES, B, C])
        epsc = sb("epsc", [P, 2])
        blank = sb("blank", [P, 512], BF16)
        lno = sb("lno", [P, N])
        t0 = sb("t0", [P, N])
        st6, st2, gst, gtm = sb("st6", [P, 6]), sb("st2", [P, 2]), sb("gst", [P, 2]), sb("gtm", [P, 8])
        xn = sb("xn", [P, N])
        q1, k1 = sb("q1", [P, N]), sb("k1", [P, N])
        v1 = sb("v1", [P, HALVES, P])
        p1 = sb("p1", [P, 4, N])
        nm1, sm1, rm1 = sb("nm1", [P, 4]), sb("sm1", [P, 4]), sb("rm1", [P, 4])
        pn1 = sb("pn1", [P, 4, N])
        pt1 = sb("pt1", [P, B, HALVES, N])
        o1 = sb("o1", [P, N])
        t1 = sb("t1", [P, N])
        x2 = sb("x2", [P, N])
        kp, vp = sb("kp", [P, 3, N + 2 * PADT]), sb("vp", [P, 3, N + 2 * PADT])
        qk = sb("qk", [P, 3, 3, N])
        le, le2, lw = (sb(n, [P, 3, 3, HALVES * B]) for n in ("le", "le2", "lw"))
        lmx, lsum, lrec = (sb(n, [P, 3, HALVES * B]) for n in ("lmx", "lsum", "lrec"))
        wb = sb("wb", [P, 3, 3, HALVES, P])
        wv = qk
        wa = sb("wa", [P, 3, N])
        t2 = sb("t2", [P, N])
        x3 = sb("x3", [P, B, N])
        lg, lg2, eg, pg3, cw = (sb(n, [P, 4, E]) for n in ("lg", "lg2", "eg", "pg3", "cw"))
        mg, sg, rg = sb("mg", [P, 4]), sb("sg", [P, 4]), sb("rg", [P, 4])
        top, topi, topf = sb("top", [P, 4, E]), sb("topi", [P, 4, E], U32), sb("topf", [P, 4, 2])
        ca, cb = sb("ca", [P, 4, E]), sb("cb", [P, 4, E])
        cwp = sb("cwp", [P, 4, 3, E], BF16)
        cr1, cr2 = sb("cr1", [P, 4, E]), sb("cr2", [P, 4, E])
        idb = sb("idb", [P, P], BF16)
        oneh = sb("oneh", [3 * E, E * P], BF16)
        cwt = sb("cwt", [3 * E, B * N], BF16)
        cwf = sb("cwf", [E, B * N])
        hg = sb("hg", [P, E, B * N])
        hw = sb("hw", [P, 3, B * N])
        t3 = sb("t3", [P, N])
        x4 = sb("x4", [P, N])
        qt4 = sb("qt4", [P, N])
        sdf = sb("sdf", [P, P])
        wsig = sb("wsig", [P, N])
        junk = sb("junk", [P, 16])
        cc = sb("cc", [P, N])
        cc2 = sb("cc2", [P, N])
        t4 = sb("t4", [P, N])
        x5 = sb("x5", [P, N + 3 * CHUNK])
        vparts, vlead = sb("vparts", [P, 3, 3, P], BF16), sb("vlead", [P, 3, P], F16)
        vsc, vr1, vr2 = (sb(n, [P, 3 * P]) for n in ("vsc", "vr1", "vr2"))
        ones = sb("ones", [P, CHUNK])
        gi, go, gos = sb("gi", [P, 1]), sb("go", [P, 2]), sb("gos", [P, 1])
        cell, hc = sb("cell", [P, 1]), sb("hc", [P, 1])
        ha, hb = sb("ha", [P, 1], F16), sb("hb", [P, 1], F16)
        hs = sb("hs", [P, N + STEPS_IN_BODY])
        ysum = sb("ysum", [P, N])
        ytm = sb("ytm", [P, HALVES, B, C])

        ident = c("ident")
        dif_bank, var_bank, rs_bank = ({n: bank[3 * (n == 5) + i] for n in range(1, 6)} for i in (0, 1, 2))
        up_bank, weight_bank = (bank[0], bank[1], bank[5]), (bank[2], bank[3], bank[6])
        v2_bank = (bank[6], bank[7], bank[0])
        UNITS = [(b, qt, pair) for qt in range(HALVES) for b in range(B) for pair in range(HEADS // 2)]
        NU = len(UNITS)
        gt, tc = bank[6][:, 0:1], bank[7][:, 0:1]

        block = ctx.enter_context(nc.Block())

        @block.sync
        def _(sp):
            for b in range(B):
                sp.dma_start(xtm[:, :, b], x[b].rearrange("(h p) c -> p h c", h=HALVES)).then_inc(on("x_in"), 16)
            sp.dma_start(cst[:], const).then_inc(on("const_in"), 16)
            sp.dma_start(bnd[:], bands).then_inc(on("bands_in"), 16)
            sp.dma_start(bias[:, 1], positions[:, 1]).then_inc(on("bias_in1"), 16)
            for w, name, dram in ((ltr, "later_in", later), (w1s, "w1_in", w1), (w2s, "w2_in", w2), (w3s, "w3_in", w3),
                                  (w5s, "w5_in", w5), (w4s, "w4_in", w4)):
                sp.dma_start(w[:], dram).then_inc(on(name), 16)
            for h in range(HALVES):
                sp.wait_ge(on("y_tm"), h + 1)
                sp.dma_start(out[:, h * P:(h + 1) * P, :].rearrange("b p c -> p b c"), ytm[:, h]).then_inc(on("out"), 16)
            sp.wait_ge(on("out"), 16 * HALVES)

        @block.gpsimd
        def _(pool):
            pool.memset(q0[:], 0.0).then_inc(on("q0_zero"), 1)
            pool.memset(vch[:], 0.0).then_inc(on("vch_zero"), 1)
            pool.memset(blank[:], 0.0).then_inc(on("blank_set"), 1)
            pool.memset(kp[:], 0.0).then_inc(on("kpad_zero"), 1)
            pool.memset(vp[:], 0.0).then_inc(on("vpad_zero"), 1)
            pool.memset(x5[:], 0.0).then_inc(on("x5_zero"), 1)
            pool.memset(x3[:], 0.0).then_inc(on("x3_zero"), 1)
            pool.memset(ones[:], 1.0).then_inc(on("ones_set"), 1)
            pool.memset(epsc[:, 0:1], 1e-5).then_inc(on("eps_set"), 1)
            pool.memset(epsc[:, 1:2], 1e-3).then_inc(on("eps_set"), 1)
            for qt in range(HALVES):
                pool.wait_ge(on("bias_in%d" % qt), 16)
                if qt == 0:
                    pool.wait_ge(on("bands_in"), 16)
                for h in range(HEADS):
                    pool.tensor_tensor(bias[:, qt, h], c("band")[:, qt * KEYS:(qt + 1) * KEYS], bias[:, qt, h],
                                       ALU.subtract).then_inc(on("bias_ready"), 1)
            pool.wait_ge(on("const_in"), 16)
            pool.tensor_copy(idb[:], ident).then_inc(on("idb_ready"), 1)
            pool.wait_ge(on("later_in"), 16)
            pool.tensor_copy(oneh[:], c("onehot")[0:3 * E]).then_inc(on("oneh_ready"), 1)
            pool.wait_ge(on("w5_in"), 16)
            vw = w5s[:, 3 * P:6 * P]
            flat = vparts[:].rearrange("p a g m -> p a (g m)")
            pool.tensor_scalar(vsc[:], vw, 1.0 / HSCALE, None, ALU.mult).then_inc(on("v_split"), 1)
            pool.wait_ge(on("v_split"), 1)
            pool.tensor_copy(vlead[:].rearrange("p g m -> p (g m)"), vsc[:]).then_inc(on("v_lead"), 1)
            pool.tensor_copy(flat[:, 0], vsc[:]).then_inc(on("v_split"), 1)
            pool.wait_ge(on("v_split"), 2)
            pool.tensor_tensor(vr1[:], vsc[:], flat[:, 0], ALU.subtract).then_inc(on("v_split"), 1)
            pool.wait_ge(on("v_split"), 3)
            pool.tensor_copy(flat[:, 1], vr1[:]).then_inc(on("v_split"), 1)
            pool.wait_ge(on("v_split"), 4)
            pool.tensor_tensor(vr2[:], vr1[:], flat[:, 1], ALU.subtract).then_inc(on("v_split"), 1)
            pool.wait_ge(on("v_split"), 5)
            pool.tensor_copy(flat[:, 2], vr2[:]).then_inc(on("v_parts"), 1)

        @block.scalar
        def _(act):
            asked = [0]

            def ask_table(function):
                asked[0] += 1
                act.activation(junk[:, asked[0]:asked[0] + 1], epsc[:, 0:1], function).then_inc(on("table"), 1)

            act.dma_start(w0s[:], w0).then_inc(on("w0_in"), 16)
            act.dma_start(vcs[:], vec).then_inc(on("vec_in"), 16)
            act.dma_start(bias[:, 0], positions[:, 0]).then_inc(on("bias_in0"), 16)
            act.wait_ge(on("g1_mm"), 1)
            act.wait_ge(on("vec_in"), 16)
            act.activation(g1[:], bank[3][0:32, 0:N], ACT.Relu, bias=v("g1b")[0:32]).then_inc(on("g1_ready"), 1)
            act.wait_ge(on("vch_zero"), 1)
            act.wait_ge(on("v0_mm"), 4)
            act.activation(vch[:, :, :, 0:HD].rearrange("p a h d -> p (a h) d"),
                           bank[2][0:KCH, :].rearrange("p (a d) -> p a d", d=HD), ACT.Copy).then_inc(on("vch"), 1)
            act.wait_ge(on("g2_mm"), 1)
            act.wait_ge(on("g2bh"), 1)
            act.activation(gateh[:], bank[7][:, 0:N], ACT.Tanh, bias=g2bh[:], scale=0.5).then_inc(on("gateh"), 1)

            def numerators(u):
                act.wait_ge(on("neg_max"), 2 * u + 2)
                if u >= 5:
                    act.wait_ge(on("p_turned"), u - 4)
                for h in range(2):
                    k = 2 * u + h
                    act.activation(pr[:, u % 5, h], sc[:, u % 4, h], ACT.Exp, bias=nmx[:, k:k + 1], scale=-1.0,
                                   accum_out=sums[:, k:k + 1]).then_inc(on("p_ready"), 1)

            def turned_copy(u):
                act.wait_ge(on("p_turned"), u + 1)
                if u >= 3:
                    act.wait_ge(on("pv_mm"), u - 2)
                act.activation(pt[:, u % 3].rearrange("p a c -> p (a c)"), bank[4 + u % 2][0:KCH, :], ACT.Copy)\
                   .then_inc(on("pt_ready"), 1)

            for u in range(NU + 3):
                if u < NU:
                    numerators(u)
                if u >= 3:
                    turned_copy(u - 3)
            act.wait_ge(on("pv_mm"), NU)
            act.activation(of[:, 1], bank[7][:], ACT.Identity, bias=v("bv0_1")).then_inc(on("of1"), 1)

            def root(n):
                ask_table(ACT.Sqrt)
                act.wait_ge(on("dif_mm"), n)
                act.activation(sq[:], dif_bank[n][:, 0:N], ACT.Square).then_inc(on("squares"), 1)
                act.wait_ge(on("var_mm"), n)
                act.wait_ge(on("eps_set"), 2)
                act.activation(sd[:].rearrange("p h b -> p (h b)"), var_bank[n][:, 0:HALVES * B], ACT.Sqrt,
                               bias=epsc[:, 0:1]).then_inc(on("root"), 1)

            root(1)
            act.wait_ge(on("gvar"), 1)
            act.activation(gtm[:, 2:3], gtm[:, 1:2], ACT.Sqrt, scale=-1.0, bias=epsc[:, 1:2]).then_inc(on("gsd"), 1)
            act.wait_ge(on("k1_mm"), 1)
            act.activation(k1[:], bank[1][:, 0:N], ACT.Identity, bias=v("bk1")).then_inc(on("k1"), 1)
            act.wait_ge(on("v1_mm"), 1)
            act.activation(v1[:].rearrange("p a c -> p (a c)"), bank[6][:, 0:N], ACT.Copy).then_inc(on("v1"), 1)
            for u in range(4):
                act.wait_ge(on("neg_max1"), u + 1)
                act.activation(p1[:, u], bank[2 + u][:, 0:N], ACT.Exp, bias=nm1[:, u:u + 1], scale=-1.0,
                               accum_out=sm1[:, u:u + 1]).then_inc(on("p1_ready"), 1)
            act.wait_ge(on("p1_turned"), 4)
            act.activation(pt1[:, 1].rearrange("p a c -> p (a c)"), bank[0][:], ACT.Copy).then_inc(on("pt1_1"), 1)
            root(2)
            act.wait_ge(on("kpad_zero"), 1)
            act.wait_ge(on("vpad_zero"), 1)
            for d in range(3):
                act.wait_ge(on("qkv2_mm"), 2 * d + 1)
                act.activation(kp[:, d, PADT:PADT + N], bank[d][:, 0:N], ACT.Copy).then_inc(on("k2_ready"), 1)
            ask_table(ACT.Exp)
            act.wait_ge(on("shifted"), 1)
            act.activation(le2[:], le[:], ACT.Exp).then_inc(on("e2_ready"), 1)
            for d in range(3):
                act.wait_ge(on("qkv2_mm"), 7 + d)
                act.activation(vp[:, d, PADT:PADT + N], v2_bank[d][:, 0:N], ACT.Copy).then_inc(on("v2_ready"), 1)
            root(3)
            act.wait_ge(on("lg2"), 1)
            act.activation(eg[:], lg2[:], ACT.Exp).then_inc(on("eg"), 1)
            for e in range(E):
                act.wait_ge(on("up_mm"), e + 1)
                act.activation(hg[:, e], up_bank[e % 3][:], ACT.Gelu, bias=v(f"b1_{e}")).then_inc(on("gelu"), 1)
            act.wait_ge(on("cw_turned"), 1)
            act.activation(cwf[:], bank[4][0:E, 0:B * N], ACT.Copy).then_inc(on("cwf"), 1)
            root(4)
            ask_table(ACT.Sigmoid)
            act.wait_ge(on("fc_mm"), 1)
            act.activation(qt4[:], bank[2][:, 0:N], ACT.Tanh, bias=v("fcb")).then_inc(on("qt4"), 1)
            act.wait_ge(on("score_mm"), 1)
            act.activation(wsig[:], bank[3][:, 0:N], ACT.Sigmoid).then_inc(on("wsig"), 1)
            root(5)
            ask_table(ACT.Sigmoid)

            with act.Fori(0, N, STEPS_IN_BODY) as base:
                for u in range(STEPS_IN_BODY):
                    t, pre, at = base + u, (u // CHUNK) * 3, u % CHUNK
                    act.wait_ge(on("i_pre"), t + 1)
                    act.activation(gi[:], bank[pre + 1][:, at:at + 1], ACT.Sigmoid)
                    act.wait_ge(on("g_pre"), t + 1)
                    act.activation(gt, bank[pre][:, at:at + 1], ACT.Tanh).then_inc(on("gates"), 1)
                    act.wait_ge(on("o_pre"), t + 1)
                    act.wait_ge(on("hc_ready"), t + 1)
                    act.activation(go[:, u % 2:u % 2 + 1], bank[pre + 2][:, at:at + 1], ACT.Sigmoid)\
                       .then_inc(on("o_gate"), 1)
                    act.wait_ge(on("gates"), t + 1)
                    act.activation(tc, gt, ACT.Tanh, scale=gi[:], bias=hc[:]).then_inc(on("tanh_c"), 1)

        @block.tensor
        def _(pe):
            mm = pe.matmul

            def keep_clock(free_bank, n):
                for _ in range(n):
                    mm(free_bank[:], blank[:, 0:P], blank[:], start=True, stop=True, skip_group_check=True)

            pe.wait_ge(on("x_in"), 16 * HALVES)
            pe.wait_ge(on("const_in"), 16)
            for h in range(HALVES):
                pe.transpose(bank[7][:, h * P:(h + 1) * P], xtm[:, h].rearrange("p b c -> p (b c)"), ident)\
                  .then_inc(on("x_turned"), 1)
            pe.wait_ge(on("w0_in"), 16)
            pe.wait_ge(on("xf"), 1)
            mm(bank[0][:, 0:N], cols(w0s, W0, "q"), xf[:], start=True, stop=True).then_inc(on("q0_mm"), 1)
            mm(bank[1][:, 0:N], cols(w0s, W0, "k"), xf[:], start=True, stop=True).then_inc(on("k0_mm"), 1)
            mm(bank[3][0:32, 0:N], cols(w0s, W0, "g1"), xf[:], start=True, stop=True).then_inc(on("g1_mm"), 1)
            for qt in range(HALVES):
                for ch in range(2):
                    at = KROW0[qt] * SIDE + ch * KCH
                    mm(bank[2][0:KCH, (2 * qt + ch) * P:(2 * qt + ch + 1) * P], xf[:, at:at + KCH],
                       cols(w0s, W0, "v"), start=True, stop=True).then_inc(on("v0_mm"), 1)

            def scores(u):
                b, qt, pair = UNITS[u]
                at = KROW0[qt] * SIDE
                if u >= 4:
                    pe.wait_ge(on("neg_max"), 2 * (u - 3))
                else:
                    pe.wait_ge(on("km"), 2 * pair + 2)
                if u == 2:
                    pe.wait_ge(on("vch"), 1)
                mm(bank[u % 4][:, 0:2 * KEYS], q0[:, b, qt * P:(qt + 1) * P],
                   km[:, 2 * pair:2 * pair + 2, at:at + KEYS], start=True, stop=True).then_inc(on("s_mm"), 1)

            def turn(u):
                pe.wait_ge(on("normalised"), u + 1)
                if u >= 2:
                    pe.wait_ge(on("pt_ready"), u - 1)
                for h in range(2):
                    for ch in range(2):
                        m = pe.transpose(bank[4 + u % 2][0:KCH, (2 * h + ch) * P:(2 * h + ch + 1) * P],
                                         pr[:, u % 5, h, ch * KCH:(ch + 1) * KCH], ident)
                m.then_inc(on("p_turned"), 1)

            def values(u):
                b, qt, pair = UNITS[u]
                pe.wait_ge(on("pt_ready"), u + 1)
                for h in range(2):
                    g, j = divmod(2 * pair + h, 4)
                    for ch in range(2):
                        m = mm(bank[6 + g][32 * j:32 * (j + 1), (b * HALVES + qt) * P:(b * HALVES + qt + 1) * P],
                               vch[:, 2 * qt + ch, b * HEADS + 2 * pair + h], pt[:, u % 3, 2 * h + ch],
                               start=(ch == 0), stop=(ch == 1))
                m.then_inc(on("pv_mm"), 1)

            pe.wait_ge(on("q0"), B)
            for u in range(NU + 5):
                if u < NU:
                    scores(u)
                if u == 1:
                    pe.wait_ge(on("g1_ready"), 1)
                    mm(bank[7][:, 0:N], cols(w0s, W0, "g2")[0:32], g1[:], start=True, stop=True).then_inc(on("g2_mm"), 1)
                if 3 <= u < NU + 3:
                    turn(u - 3)
                if u == 5:
                    pe.wait_ge(on("gateh"), 1)
                if u >= 5:
                    values(u - 5)
            pe.wait_ge(on("blank_set"), 1)
            keep_clock(bank[4], 3)
            for g in range(2):
                pe.wait_ge(on(f"of{g}"), 1)
                for b in range(B):
                    m = mm(bank[1][b * C:(b + 1) * C, 0:N], cols(w0s, W0, f"proj{g}"), of[:, g, b * N:(b + 1) * N],
                           start=(g == 0), stop=(g == 1), skip_group_check=True)
            m.then_inc(on("proj0_mm"), 1)
            keep_clock(bank[4], 3)

            def b_part(parity, k):
                return mm(bank[3 * parity + k][:, 0:CHUNK], w5s[:, (6 + k) * P:(7 + k) * P], ones[:],
                          start=True, stop=False, skip_group_check=True)

            def norm(n, src):
                mm(dif_bank[n][:, 0:N], c("centre"), src, start=True, stop=True).then_inc(on("dif_mm"), 1)
                keep_clock(rs_bank[n], 2)
                if n < 5:
                    keep_clock(rs_bank[n], 1)
                else:
                    b_part(0, 0)
                pe.wait_ge(on("squares"), n)
                for h in range(HALVES):
                    m = mm(var_bank[n][:, h * B:(h + 1) * B], sq[:, h * P:(h + 1) * P], c("means"), start=True, stop=True)
                m.then_inc(on("var_mm"), 1)
                if n == 5:
                    b_part(0, 1)
                    b_part(0, 2)
                keep_clock(rs_bank[n], 3)
                pe.wait_ge(on("rs"), n)
                for h in range(HALVES):
                    m = pe.transpose(rs_bank[n][:, h * P:(h + 1) * P], rsw[:, h].rearrange("p b c -> p (b c)"), ident)
                m.then_inc(on("rs_mm"), 1)
                keep_clock(var_bank[n], 2)

            pe.wait_ge(on("y0"), 1)
            norm(1, y0[:])
            keep_clock(bank[1], 4)
            pe.wait_ge(on("later_in"), 16)
            pe.wait_ge(on("gst"), 1)
            mm(bank[2][:, 0:2], c("group"), gst[:], start=True, stop=True).then_inc(on("group_mm"), 1)
            keep_clock(bank[1], 7)
            pe.wait_ge(on("w1_in"), 16)
            pe.wait_ge(on("xn"), 1)
            mm(bank[0][:, 0:N], cols(w1s, W1, "q"), xn[:], start=True, stop=True).then_inc(on("q1_mm"), 1)
            mm(bank[1][:, 0:N], cols(w1s, W1, "k"), xn[:], start=True, stop=True).then_inc(on("k1_mm"), 1)
            for h in range(HALVES):
                m = mm(bank[6][:, h * P:(h + 1) * P], xn[:, h * P:(h + 1) * P], cols(w1s, W1, "v"),
                       start=True, stop=True)
            m.then_inc(on("v1_mm"), 1)
            pe.wait_ge(on("q1"), 1)
            pe.wait_ge(on("k1"), 1)
            for u in range(4):
                b, qt = u // 2, u % 2
                r = slice(b * C, (b + 1) * C)
                mm(bank[2 + u][:, 0:N], q1[r, qt * P:(qt + 1) * P], k1[r, :], start=True, stop=True)\
                    .then_inc(on("s1_mm"), 1)
            keep_clock(bank[1], 5)
            for u in range(4):
                b, qt = u // 2, u % 2
                pe.wait_ge(on("pn1"), u + 1)
                for ch in range(HALVES):
                    m = pe.transpose((bank[7] if b == 0 else bank[0])[:, ch * N + qt * P:ch * N + (qt + 1) * P],
                                     pn1[:, u, ch * P:(ch + 1) * P], ident)
                m.then_inc(on("p1_turned"), 1)
            pe.wait_ge(on("v1"), 1)
            keep_clock(bank[6], 3)
            for b in range(B):
                pe.wait_ge(on(f"pt1_{b}"), 1)
                for ch in range(HALVES):
                    m = mm(bank[1][b * C:(b + 1) * C, 0:N], v1[:, ch, b * C:(b + 1) * C], pt1[:, b, ch],
                           start=(ch == 0), stop=(ch == 1))
            m.then_inc(on("o1_mm"), 1)
            keep_clock(bank[6], 2)
            pe.wait_ge(on("o1"), 1)
            mm(bank[2][:, 0:N], cols(w1s, W1, "p"), o1[:], start=True, stop=True).then_inc(on("proj1_mm"), 1)
            keep_clock(bank[6], 2)
            pe.wait_ge(on("t1"), 1)
            norm(2, t1[:])

            pe.wait_ge(on("w2_in"), 16)
            pe.wait_ge(on("x2"), 1)
            for d in range(3):
                mm(bank[d][:, 0:N], cols(w2s, W2, f"k{d}"), x2[:], start=True, stop=True).then_inc(on("qkv2_mm"), 1)
                mm(bank[3 + d][:, 0:N], cols(w2s, W2, f"q{d}"), x2[:], start=True, stop=True).then_inc(on("qkv2_mm"), 1)
            pe.wait_ge(on("k2_ready"), 2)
            for n in range(9):
                pe.wait_ge(on("qk"), n + 1)
                for h in range(HALVES):
                    m = mm(bank[1][:, (n * HALVES + h) * B:(n * HALVES + h + 1) * B], qk[:, n // 3, n % 3, h * P:(h + 1) * P],
                           c("eighths"), start=True, stop=True)
            m.then_inc(on("logit_mm"), 1)
            for d in range(3):
                mm(v2_bank[d][:, 0:N], cols(w2s, W2, f"v{d}"), x2[:], start=True, stop=True).then_inc(on("qkv2_mm"), 1)
            keep_clock(bank[2], 3)
            for n in range(9):
                d, j = divmod(n, 3)
                pe.wait_ge(on("wb"), d + 1)
                if n >= 4:
                    pe.wait_ge(on("wv"), n - 3)
                for h in range(HALVES):
                    m = pe.transpose(bank[2 + n % 4][:, h * P:(h + 1) * P], wb[:, d, j, h], ident)
                m.then_inc(on("w_turned"), 1)
            for d in range(3):
                pe.wait_ge(on("wa"), d + 1)
                mm(bank[6][:, 0:N], cols(w2s, W2, "proj"), wa[:, d], start=(d == 0), stop=False)
                pe.wait_ge(on("wv"), 3 * d + 3)
                m = mm(bank[6][:, 0:N], cols(w2s, W2, "proj"), wv[:, d, 2], start=False, stop=(d == 2))
            m.then_inc(on("proj2_mm"), 1)
            keep_clock(bank[2], 2)
            pe.wait_ge(on("t2"), 1)
            norm(3, t2[:])

            pe.wait_ge(on("w3_in"), 16)
            pe.wait_ge(on("x3"), B)
            for h in range(HALVES):
                for b in range(B):
                    u = h * B + b
                    m = mm(bank[2][:, u * E:(u + 1) * E], x3[:, b, h * P:(h + 1) * P], cols(w3s, W3, "gate"),
                           start=True, stop=True)
            m.then_inc(on("gate_mm"), 1)

            def up(e):
                if e >= 3:
                    pe.wait_ge(on("gelu"), e - 2)
                mm(up_bank[e % 3][:], cols(w3s, W3, "up")[:, e * HID:(e + 1) * HID], x3[:].rearrange("p b n -> p (b n)"),
                   start=True, stop=True).then_inc(on("up_mm"), 1)

            def spread_weight(e):
                if e >= 3:
                    pe.wait_ge(on("weighted"), e - 2)
                mm(weight_bank[e % 3][:], oneh[:, e * P:(e + 1) * P], cwt[:], start=True, stop=True).then_inc(on("cw_mm"), 1)

            def down(e):
                pe.wait_ge(on("weighted"), e + 1)
                for b in range(B):
                    m = mm(bank[7][b * C:(b + 1) * C, 0:N], cols(w3s, W3, "down")[:, e * C:(e + 1) * C],
                           hw[:, e % 3, b * N:(b + 1) * N], start=(e == 0), stop=False, skip_group_check=True)
                m.then_inc(on("down_mm"), 1)

            for e in range(UP_FIRST):
                up(e)
            pe.wait_ge(on("idb_ready"), 1)
            pe.wait_ge(on("cw_parts"), 3)
            cwb = bank[3][:].bitcast(BF16)
            for h in range(HALVES):
                for b in range(B):
                    u, at = h * B + b, b * N + h * P
                    pe.transpose(cwb[0:3 * E, at:at + P], cwp[:, u].rearrange("p a e -> p (a e)"), idb[:])
                    m = pe.transpose(bank[4][0:E, at:at + P], cw[:, u], ident)
            m.then_inc(on("cw_turned"), 1)
            up(UP_FIRST)
            pe.wait_ge(on("cwt"), 1)
            pe.wait_ge(on("oneh_ready"), 1)
            spread_weight(0)
            for e in range(E):
                if e + 1 < E:
                    spread_weight(e + 1)
                if e + UP_FIRST + 1 < E:
                    up(e + UP_FIRST + 1)
                if e >= 1:
                    down(e - 1)
            pe.wait_ge(on("cwf"), 1)
            for b in range(B):
                mm(bank[7][b * C:(b + 1) * C, 0:N], cols(w3s, W3, "b2")[0:E], cwf[:, b * N:(b + 1) * N],
                   start=False, stop=False, skip_group_check=True)
            down(E - 1)
            pe.wait_ge(on("t3"), 1)
            norm(4, t3[:])

            pe.wait_ge(on("w4_in"), 16)
            pe.wait_ge(on("x4"), 1)
            mm(bank[2][:, 0:N], cols(w4s, W4, "fc"), x4[:], start=True, stop=True).then_inc(on("fc_mm"), 1)
            mm(bank[4][:, 0:N], c("dup0"), x4[:], start=True, stop=True)
            mm(bank[5][:, 0:N], c("diff"), x4[:], start=True, stop=True).then_inc(on("dup_mm"), 1)
            pe.wait_ge(on("sdf"), 1)
            pe.wait_ge(on("qt4"), 1)
            mm(bank[3][:, 0:N], sdf[:], qt4[:], start=True, stop=True).then_inc(on("score_mm"), 1)
            keep_clock(bank[7], 4)
            pe.wait_ge(on("w5_in"), 16)
            pe.wait_ge(on("ones_set"), 1)
            pe.wait_ge(on("t4"), 1)
            norm(5, t4[:])

            def x_part(parity, k, start):
                return mm(bank[3 * parity + k][:, 0:CHUNK], w5s[:, k * P:(k + 1) * P], x5[:, bass.ds(start, CHUNK)],
                          start=False, stop=False, skip_group_check=True)

            def recur(parity, k, at, parts, h):
                for weight in parts:
                    m = mm(bank[3 * parity + k][:, at:at + 1], weight, h, start=False, stop=False, skip_group_check=True)
                return m

            pe.wait_ge(on("v_parts"), 1)
            pe.wait_ge(on("v_lead"), 1)
            pe.wait_ge(on("x5"), 1)
            for k in (1, 0, 2):
                x_part(0, k, 0)
            with pe.Fori(0, N, STEPS_IN_BODY) as base:
                for u in range(STEPS_IN_BODY):
                    t, parity, at = base + u, u // CHUNK, u % CHUNK
                    pe.wait_ge(on("ha_ready"), t + 1)
                    for k in (1, 0, 2):
                        recur(parity, k, at, [vparts[:, a, k] for a in range(3)], ha[:])
                    pe.wait_ge(on("hb_ready"), t + 1)
                    recur(parity, 1, at, [vlead[:, 1]], hb[:]).then_inc(on("i_pre"), 1)
                    recur(parity, 0, at, [vlead[:, 0]], hb[:]).then_inc(on("g_pre"), 1)
                    recur(parity, 2, at, [vlead[:, 2]], hb[:]).then_inc(on("o_pre"), 1)
                    if at < 3:
                        b_part(1 - parity, at)
                    elif at < 6:
                        x_part(1 - parity, at - 3, base + (parity + 1) * CHUNK)
            pe.wait_ge(on("ysum"), 1)
            for h in range(HALVES):
                pe.transpose(bank[h][:, 0:P], ysum[:, h * P:(h + 1) * P], ident).then_inc(on("y_turned"), 1)

        @block.vector
        def _(dve):
            tt, ts, stt = dve.tensor_tensor, dve.tensor_scalar, dve.scalar_tensor_tensor
            links = [0]

            def link(ins):
                links[0] += 1
                ins.then_inc(on("dve_link"), 1)
                dve.wait_ge(on("dve_link"), links[0])

            dve.wait_ge(on("x_turned"), HALVES)
            dve.tensor_copy(xf[:], bank[7][:, 0:N]).then_inc(on("xf"), 1)
            dve.wait_ge(on("vec_in"), 16)
            ts(g2bh[:], v("g2b"), 0.5, None, ALU.mult).then_inc(on("g2bh"), 1)
            dve.wait_ge(on("q0_mm"), 1)
            dve.wait_ge(on("q0_zero"), 1)
            for b in range(B):
                r = slice(b * C, (b + 1) * C)
                ts(q0[r, b], bank[0][r, 0:N], v("bq0")[r], -(HD ** -0.5), ALU.add, ALU.mult).then_inc(on("q0"), 1)
            dve.wait_ge(on("k0_mm"), 1)
            link(ts(k0[:], bank[1][:, 0:N], v("bk0"), None, ALU.add))
            for h in range(HEADS):
                ts(km[:, h], k0[:], c("heads")[:, h:h + 1], None, ALU.mult).then_inc(on("km"), 1)

            def row_min(u):
                b, qt, pair = UNITS[u]
                dve.wait_ge(on("s_mm"), u + 1)
                dve.wait_ge(on("bias_ready"), qt * HEADS + 2 * pair + 2)
                if u >= 4:
                    dve.wait_ge(on("p_ready"), 2 * (u - 3))
                for h in range(2):
                    k = 2 * u + h
                    dve.tensor_tensor_reduce(sc[:, u % 4, h], bank[u % 4][:, h * KEYS:(h + 1) * KEYS],
                                             bias[:, qt, 2 * pair + h], 1.0, 3.0e38, ALU.add, ALU.min,
                                             nmx[:, k:k + 1]).then_inc(on("neg_max"), 1)

            def normalise(u):
                k = 2 * u
                dve.wait_ge(on("p_ready"), k + 2)
                link(dve.reciprocal(rsum[:, k:k + 2], sums[:, k:k + 2]))
                for h in range(2):
                    m = ts(pr[:, u % 5, h], pr[:, u % 5, h], rsum[:, k + h:k + h + 1], None, ALU.mult)
                m.then_inc(on("normalised"), 1)

            for u in range(NU + 1):
                if u < NU:
                    row_min(u)
                if u >= 1:
                    normalise(u - 1)
            dve.wait_ge(on("gateh"), 1)
            ts(gate[:], gateh[:], 0.5, 0.5, ALU.mult, ALU.add).then_inc(on("gate"), 1)
            dve.wait_ge(on("pv_mm"), NU - 2)
            ts(of[:, 0], bank[6][:], v("bv0_0"), None, ALU.add).then_inc(on("of0"), 1)
            dve.wait_ge(on("proj0_mm"), 1)
            dve.wait_ge(on("gate"), 1)
            link(stt(out=pg[:], in0=bank[1][:, 0:N], scalar=v("bp0"), in1=gate[:], op0=ALU.add, op1=ALU.mult))
            tt(y0[:], pg[:], xf[:], ALU.add).then_inc(on("y0"), 1)

            def norm(n, dst, done):
                dve.wait_ge(on("squares"), n)
                dve.tensor_copy(dif[:], dif_bank[n][:, 0:N]).then_inc(on("dif"), 1)
                dve.wait_ge(on("root"), n)
                link(dve.reciprocal(rs[:], sd[:]))
                dve.tensor_copy(rsw[:], rs[:][:, :, :, None].broadcast_to([P, HALVES, B, C])).then_inc(on("rs"), 1)
                dve.wait_ge(on("rs_mm"), n)
                dve.wait_ge(on("dif"), n)
                if n == 3:
                    dve.wait_ge(on("x3_zero"), 1)
                    for b in range(B):
                        r = slice(b * C, (b + 1) * C)
                        tt(dst[r, b], dif[r, :], rs_bank[n][r, 0:N], ALU.mult).then_inc(on(done), 1)
                else:
                    tt(dst, dif[:], rs_bank[n][:, 0:N], ALU.mult).then_inc(on(done), 1)

            norm(1, lno[:], "lno")
            dve.wait_ge(on("lno"), 1)
            ts(t0[:], lno[:], v("lng"), v("lnb"), ALU.mult, ALU.add).then_inc(on("t0"), 1)
            dve.wait_ge(on("t0"), 1)
            link(dve.bn_stats(st6[:], t0[:]))
            link(dve.bn_aggr(st2[:], st6[:]))
            dve.tensor_copy(gst[:, 0:1], st2[:, 0:1]).then_inc(on("gst_mean"), 1)
            stt(out=gst[:, 1:2], in0=st2[:, 0:1], scalar=st2[:, 0:1], in1=st2[:, 1:2], op0=ALU.mult, op1=ALU.add)\
                .then_inc(on("gst"), 1)
            dve.wait_ge(on("group_mm"), 1)
            link(dve.tensor_copy(gtm[:, 6:8], bank[2][:, 0:2]))
            stt(out=gtm[:, 1:2], in0=gtm[:, 6:7], scalar=gtm[:, 6:7], in1=gtm[:, 7:8], op0=ALU.mult, op1=ALU.subtract)\
                .then_inc(on("gvar"), 1)
            dve.wait_ge(on("gsd"), 1)
            link(dve.reciprocal(gtm[:, 3:4], gtm[:, 2:3]))
            link(tt(gtm[:, 4:5], gtm[:, 3:4], v("gamma"), ALU.mult))
            link(ts(lno[:], t0[:], gtm[:, 6:7], gtm[:, 4:5], ALU.subtract, ALU.mult))
            ts(xn[:], lno[:], v("beta"), None, ALU.add).then_inc(on("xn"), 1)
            dve.wait_ge(on("q1_mm"), 1)
            ts(q1[:], bank[0][:, 0:N], v("bq1"), -(C ** -0.5), ALU.add, ALU.mult).then_inc(on("q1"), 1)
            for u in range(4):
                dve.wait_ge(on("s1_mm"), u + 1)
                dve.tensor_reduce(nm1[:, u:u + 1], bank[2 + u][:, 0:N], AX.X, ALU.min).then_inc(on("neg_max1"), 1)
            for u in range(5):
                if u < 4:
                    dve.wait_ge(on("p1_ready"), u + 1)
                    dve.reciprocal(rm1[:, u:u + 1], sm1[:, u:u + 1]).then_inc(on("rm1"), 1)
                if u >= 1:
                    dve.wait_ge(on("rm1"), u)
                    ts(pn1[:, u - 1], p1[:, u - 1], rm1[:, u - 1:u], None, ALU.mult).then_inc(on("pn1"), 1)
            dve.wait_ge(on("p1_turned"), 2)
            dve.tensor_copy(pt1[:, 0].rearrange("p a c -> p (a c)"), bank[7][:]).then_inc(on("pt1_0"), 1)
            dve.wait_ge(on("o1_mm"), 1)
            ts(o1[:], bank[1][:, 0:N], v("bv1"), None, ALU.add).then_inc(on("o1"), 1)
            dve.wait_ge(on("proj1_mm"), 1)
            stt(out=t1[:], in0=bank[2][:, 0:N], scalar=v("bp1"), in1=xn[:], op0=ALU.add, op1=ALU.add)\
                .then_inc(on("t1"), 1)
            norm(2, x2[:], "x2")

            for d in range(3):
                dve.wait_ge(on("k2_ready"), d + 1)
                dve.wait_ge(on("qkv2_mm"), 2 * d + 2)
                for j in range(3):
                    s = PADT + (j - 1) * DIL[d]
                    tt(qk[:, d, j], bank[3 + d][:, 0:N], kp[:, d, s:s + N], ALU.mult).then_inc(on("qk"), 1)
            logits = bank[1][:, 0:9 * HALVES * B].rearrange("p (d j x) -> p d j x", d=3, j=3)
            dve.wait_ge(on("logit_mm"), 1)
            link(dve.tensor_reduce(lmx[:], logits.rearrange("p d j x -> p d x j"), AX.X, ALU.max))
            tt(le[:], logits, lmx[:][:, :, None, :].broadcast_to([P, 3, 3, HALVES * B]), ALU.subtract)\
                .then_inc(on("shifted"), 1)
            dve.wait_ge(on("e2_ready"), 1)
            link(dve.tensor_reduce(lsum[:], le2[:].rearrange("p d j x -> p d x j"), AX.X, ALU.add))
            link(dve.reciprocal(lrec[:], lsum[:]))
            for d in range(3):
                stt(out=lw[:, d], in0=le2[:, d], scalar=1.0 / len(DIL),
                    in1=lrec[:, d, None, :].broadcast_to([P, 3, HALVES * B]), op0=ALU.mult, op1=ALU.mult)\
                    .then_inc(on("lw"), 1)
            for d in range(3):
                dve.wait_ge(on("lw"), d + 1)
                dve.tensor_copy(wb[:, d].rearrange("p j h (b c) -> p (j h b) c", b=B),
                                lw[:, d].rearrange("p j x -> p (j x)")[:, :, None].broadcast_to([P, 3 * HALVES * B, C]))\
                   .then_inc(on("wb"), 1)

            def weighted_value(n):
                d, j = divmod(n, 3)
                s = PADT + (j - 1) * DIL[d]
                dve.wait_ge(on("w_turned"), n + 1)
                dve.wait_ge(on("v2_ready"), d + 1)
                tt(wv[:, d, j], bank[2 + n % 4][:, 0:N], vp[:, d, s:s + N], ALU.mult).then_inc(on("wv"), 1)

            def sum_two(d):
                dve.wait_ge(on("wv"), 3 * d + 2)
                tt(wa[:, d], wv[:, d, 0], wv[:, d, 1], ALU.add).then_inc(on("wa"), 1)

            for n in range(9):
                weighted_value(n)
                if n % 3 == 2:
                    sum_two(n // 3)
            dve.wait_ge(on("proj2_mm"), 1)
            stt(out=t2[:], in0=bank[6][:, 0:N], scalar=v("bp2"), in1=t1[:], op0=ALU.add, op1=ALU.add)\
                .then_inc(on("t2"), 1)
            norm(3, x3[:], "x3")

            dve.wait_ge(on("gate_mm"), 1)
            link(tt(lg[:], bank[2][:, 0:4 * E].rearrange("p (u e) -> p u e", e=E),
               v("gateb")[:, None, :].broadcast_to([P, 4, E]), ALU.add))
            link(dve.tensor_reduce(mg[:], lg[:], AX.X, ALU.max))
            tt(lg2[:], lg[:], mg[:][:, :, None].broadcast_to([P, 4, E]), ALU.subtract).then_inc(on("lg2"), 1)
            dve.wait_ge(on("eg"), 1)
            link(dve.tensor_reduce(sg[:], eg[:], AX.X, ALU.add))
            link(dve.reciprocal(rg[:], sg[:]))
            link(tt(pg3[:], eg[:], rg[:][:, :, None].broadcast_to([P, 4, E]), ALU.mult))
            for u in range(4):
                dve.max(top[:, u], pg3[:, u]).then_inc(on("top"), 1)
            for u in range(4):
                dve.wait_ge(on("top"), u + 1)
                m = dve.max_index(topi[:, u], top[:, u], pg3[:, u])
            link(m)
            link(dve.tensor_copy(topf[:], topi[:, :, 0:2]))
            for k, dst in ((0, ca), (1, cb)):
                tt(dst[:], c("iota")[:, None, :].broadcast_to([P, 4, E]), topf[:, :, k:k + 1].broadcast_to([P, 4, E]),
                   ALU.is_equal).then_inc(on("picked"), 1)
            for k, dst in ((0, ca), (1, cb)):
                dve.wait_ge(on("picked"), k + 1)
                m = tt(dst[:], dst[:], top[:, :, k:k + 1].broadcast_to([P, 4, E]), ALU.mult)
            link(m)
            link(tt(cw[:], ca[:], cb[:], ALU.add))
            dve.tensor_copy(cwp[:, :, 0], cw[:]).then_inc(on("cw_parts"), 1)
            dve.wait_ge(on("cw_parts"), 1)
            link(tt(cr1[:], cw[:], cwp[:, :, 0], ALU.subtract))
            dve.tensor_copy(cwp[:, :, 1], cr1[:]).then_inc(on("cw_parts"), 1)
            dve.wait_ge(on("cw_parts"), 2)
            link(tt(cr2[:], cr1[:], cwp[:, :, 1], ALU.subtract))
            dve.tensor_copy(cwp[:, :, 2], cr2[:]).then_inc(on("cw_parts"), 1)
            dve.wait_ge(on("cw_turned"), 1)
            dve.tensor_copy(cwt[:], bank[3][:].bitcast(BF16)[0:3 * E, 0:B * N]).then_inc(on("cwt"), 1)
            for e in range(E):
                dve.wait_ge(on("gelu"), e + 1)
                dve.wait_ge(on("cw_mm"), e + 1)
                if e >= 3:
                    dve.wait_ge(on("down_mm"), e - 2)
                tt(hw[:, e % 3], hg[:, e], weight_bank[e % 3][:], ALU.mult).then_inc(on("weighted"), 1)
            dve.wait_ge(on("down_mm"), E)
            tt(t3[:], bank[7][:, 0:N], t2[:], ALU.add).then_inc(on("t3"), 1)
            norm(4, x4[:], "x4")

            dve.wait_ge(on("w4_in"), 16)
            tt(sdf[:], cols(w4s, W4, "s1"), cols(w4s, W4, "s0"), ALU.subtract).then_inc(on("sdf"), 1)
            dve.wait_ge(on("dup_mm"), 1)
            tt(cc2[:], bank[4][:, 0:N], t3[:], ALU.add).then_inc(on("cc"), 1)
            dve.wait_ge(on("wsig"), 1)
            tt(cc[:], bank[5][:, 0:N], wsig[:], ALU.mult).then_inc(on("cc"), 1)
            dve.wait_ge(on("cc"), 2)
            tt(t4[:], cc[:], cc2[:], ALU.add).then_inc(on("t4"), 1)
            dve.memset(hc[:], 0.0).then_inc(on("hc_ready"), 1)
            dve.memset(ha[:], 0.0).then_inc(on("ha_ready"), 1)
            dve.memset(hb[:], 0.0).then_inc(on("hb_ready"), 1)
            dve.wait_ge(on("x5_zero"), 1)
            norm(5, x5[:, 0:N], "x5")

            with dve.Fori(0, N, STEPS_IN_BODY) as base:
                for u in range(STEPS_IN_BODY):
                    t, o = base + u, go[:, u % 2:u % 2 + 1]
                    dve.wait_ge(on("o_gate"), t + 1)
                    ts(gos[:], o, HSCALE, None, ALU.mult)
                    dve.wait_ge(on("tanh_c"), t + 1)
                    stt(out=ha[:], in0=tc, scalar=HSCALE, in1=o, op0=ALU.mult, op1=ALU.mult).then_inc(on("ha_ready"), 1)
                    stt(out=cell[:], in0=gt, scalar=gi[:], in1=hc[:], op0=ALU.mult, op1=ALU.add)
                    dve.wait_ge(on("ha_ready"), t + 2)
                    stt(out=hb[:], in0=tc, scalar=gos[:], in1=ha[:], op0=ALU.mult, op1=ALU.subtract)\
                        .then_inc(on("hb_ready"), 1)
                    tt(hs[:, bass.ds(t, 1)], tc, o, ALU.mult).then_inc(on("h_ready"), 1)
                    dve.wait_ge(on("h_ready"), t + 1)
                    tt(hc[:], hs[:, bass.ds(t, 1)], cell[:], ALU.mult).then_inc(on("hc_ready"), 1)
            dve.wait_ge(on("h_ready"), N)
            tt(ysum[:], hs[:, 0:N], t4[:], ALU.add).then_inc(on("ysum"), 1)
            for h in range(HALVES):
                dve.wait_ge(on("y_turned"), h + 1)
                dve.tensor_copy(ytm[:, h].rearrange("p b c -> p (b c)"), bank[h][:, 0:P]).then_inc(on("y_tm"), 1)


def constants(np):
    f = np.float32
    out = {}
    out["ident"] = np.eye(P, dtype=f)
    batch = np.arange(P) // C
    same = (batch[:, None] == batch[None, :]).astype(f)
    out["centre"] = np.eye(P, dtype=f) - same / C
    out["means"] = (batch[:, None] == np.arange(B)[None, :]).astype(f) / C
    groups = np.arange(P) // (C // 8)
    out["group"] = (groups[:, None] == groups[None, :]).astype(f) / (C // 8)
    out["eighths"] = (batch[:, None] == np.arange(B)[None, :]).astype(f) * C ** -0.5
    src, dst = np.arange(P)[:, None], np.arange(P)[None, :]
    out["dup0"] = ((src < C) & (dst % C == src)).astype(f)
    out["diff"] = (dst >= C) * ((src == dst).astype(f) - (src == dst - C).astype(f))
    out["heads"] = ((np.arange(P) % C) // HD)[:, None] == np.arange(HEADS)[None, :]
    out["iota"] = np.tile(np.arange(E), (P, 1))
    start = np.clip(np.arange(SIDE) - K // 2, 0, SIDE - K)
    inside = (np.arange(SIDE)[None, :] >= start[:, None]) & (np.arange(SIDE)[None, :] < start[:, None] + K)
    band = np.zeros((2, 8, SIDE, BAND, SIDE), bool)
    for qt in range(2):
        rows = inside[8 * qt:8 * qt + 8, KROW0[qt]:KROW0[qt] + BAND]
        band[qt] = rows[:, None, :, None] & inside[None, :, None, :]
    band = np.where(band, 0.0, 1e30).reshape(2, P, KEYS)
    out["band"] = band.transpose(1, 0, 2).reshape(P, 2 * KEYS)
    one = np.zeros((P, E, P))
    for e in range(E):
        one[[e, E + e, 2 * E + e], e] = 1
    out["onehot"] = one.reshape(P, E * P)
    return [np.concatenate([out[n].astype(f).reshape(P, w) for n, w in columns.items()], axis=1)
            for columns in (CONST, BANDS, LATER)]


def kernel(**inputs):
    import numpy as np
    import concourse.bacc as bacc
    from concourse.bass_utils import run_bass_kernel_spmd as run

    a = {n: np.asarray(x) for n, x in inputs.items()}

    def blocks(w):
        k, m = w.shape
        out = np.zeros((2 * k, 2 * m), w.dtype)
        out[:k, :m] = w
        out[k:, m:] = w
        return out

    def rows(w):
        return np.concatenate([w, np.zeros((P - w.shape[0], w.shape[1]), w.dtype)])

    def both(x):
        return rows(np.tile(x.reshape(-1, 1), (2, 1)))

    def spread(x):
        x = x.reshape(4, HD, -1)
        return np.pad(x, ((0, 0), (0, 32 - HD), (0, 0))).reshape(P, -1)

    def pack(columns, parts):
        return np.ascontiguousarray(np.concatenate([parts[n] for n in columns], axis=1))

    L0 = {n[8:]: x for n, x in a.items() if n.startswith("L0_conv_")}
    L1 = {n[8:]: x for n, x in a.items() if n.startswith("L1_conv_")}
    F3 = {n[7:]: x for n, x in a.items() if n.startswith("L3_ffn_")}
    zero = np.zeros((C, C), np.float32)
    s = np.tile(a["L3_attn_score_w"].reshape(C, 1), (1, C))
    qkv = L0["qkv_w"]
    wqkv = a["L2_attn_Wqkv"]
    parts = {
        "w0": pack(W0, dict(q=blocks(qkv[:, :C]), k=blocks(qkv[:, C:2 * C]), v=blocks(qkv[:, 2 * C:]),
                            g1=blocks(L0["g1_w"]), g2=rows(blocks(np.tile(L0["g2_w"], (1, C)))),
                            proj0=spread(L0["proj_w"][:P // 4]), proj1=spread(L0["proj_w"][P // 4:]))),
        "w1": pack(W1, dict(q=blocks(L1["Wq"]), k=blocks(L1["Wk"]), v=blocks(L1["Wv"]), p=blocks(L1["Wp"]))),
        "w2": pack(W2, {f"{n}{d}": blocks(wqkv[d][:, i * C:(i + 1) * C]) for d in range(3) for i, n in enumerate("qkv")}
                   | dict(proj=blocks(a["L2_attn_Wproj"]))),
        "w3": pack(W3, dict(gate=np.tile(a["L2_ffn_gate_w"], (2, 1)), b2=rows(a["L2_ffn_b2"]),
                            up=np.tile(a["L2_ffn_W1"].transpose(1, 0, 2).reshape(C, E * HID), (2, 1)),
                            down=a["L2_ffn_W2"].transpose(1, 0, 2).reshape(HID, E * C))),
        "w4": pack(W4, dict(fc=blocks(a["L3_attn_fc_w"].T),
                            s0=np.block([[zero, s], [zero, zero]]), s1=np.block([[zero, zero], [zero, s]]))),
    }
    lstm = {"g": "c", "i": "i", "o": "o"}
    parts["w5"] = pack(W5, {f"U{g}": blocks(F3[f"U_{n}"]) for g, n in lstm.items()}
                       | {f"V{g}": blocks(F3[f"V_{n}"]) for g, n in lstm.items()}
                       | {f"b{g}": rows(np.tile(F3[f"b_{n}"].reshape(1, C), (1, 2))) for g, n in lstm.items()})
    qb = L0["qkv_b"]
    vec = dict(bq0=qb[:C], bk0=qb[C:2 * C], bp0=L0["proj_b"], g1b=L0["g1_b"],
               g2b=np.repeat(L0["g2_b"], C), lng=L0["ln_g"], lnb=L0["ln_b"], gamma=L1["gamma"], beta=L1["beta"],
               bq1=L1["bq"], bk1=L1["bk"], bv1=L1["bv"], bp1=L1["bp"], bp2=a["L2_attn_bproj"], fcb=a["L3_attn_fc_b"])
    vec = {n: both(x) for n, x in vec.items()} | {f"b1_{e}": a["L2_ffn_b1"][e].reshape(HID, 1) for e in range(E)}
    vec |= {f"bv0_{g}": spread(qb[2 * C + g * C // 2:2 * C + (g + 1) * C // 2]) for g in range(2)}
    vec["gateb"] = np.tile(a["L2_ffn_gate_b"].reshape(1, E), (P, 1))
    parts["vec"] = pack(VECS, vec)
    parts["const"], parts["bands"], parts["later"] = constants(np)
    parts["x"] = np.ascontiguousarray(a["x"].reshape(B, N, C))
    rpb = np.pad(L0["rpb"], ((0, 0), (APAD, APAD), (BPAD, BPAD)))
    tiles = []
    for i in range(SIDE):
        a0, j0 = KROW0[i * HALVES // SIDE] - i + K - 1 + APAD, SIDE - 1
        tiles.append(np.stack([rpb[:, a0:a0 + BAND, j0 - j:j0 - j + SIDE].reshape(HEADS, KEYS) for j in range(SIDE)]))
    parts["positions"] = np.ascontiguousarray(np.stack(tiles).reshape(HALVES, P, HEADS, KEYS).transpose(1, 0, 2, 3))

    nc = bacc.Bacc("TRN2", target_bir_lowering=False, num_devices=1)
    order = ["x", "const", "bands", "later", "vec", "positions", "w0", "w1", "w2", "w3", "w4", "w5"]
    args = [nc.dram_tensor(f"in_{n}", parts[n].shape, mybir.dt.from_np(parts[n].dtype), kind="ExternalInput").ap()
            for n in order]
    args.append(nc.dram_tensor("out_y", (B, N, C), F32, kind="ExternalOutput").ap())
    build(nc, *args)
    r = run(nc, [{f"in_{n}": parts[n] for n in order}], core_ids=[0])
    return r.results[0]["out_y"].reshape(B, SIDE, SIDE, C)
```
